# Optimizing a Trainium2 kernel written in Bass

```python
import numpy as np
import jax
import jax.numpy as jnp

def _softmax(x, axis=-1):
    return jax.nn.softmax(x, axis=axis)

def _gelu(x):
    return jax.nn.gelu(x, approximate=True)

def _silu(x):
    return jax.nn.silu(x)

def _sigmoid(x):
    return jax.nn.sigmoid(x)

def _layernorm(x, axis=-1, eps=1e-05):
    m = jnp.mean(x, axis=axis, keepdims=True)
    v = jnp.var(x, axis=axis, keepdims=True)
    return (x - m) / jnp.sqrt(v + eps)

def _scatter_add(tgt, idx, src, axis=0):
    return tgt.at[idx].add(src)

def _segment_sum(src, seg, n):
    return jax.ops.segment_sum(src, seg, n)
kernel_name = 'mk_gnn_resnorm_d2_gnn_r8_8beab9'

def setup_inputs(seed: int=0):
    np.random.seed(seed)
    _w = jnp.asarray

    def _rec_inputs():
        import jax
        import jax.numpy as jnp
        _gk = jax.random.key(seed)
        x = -0.000202 + 1 * jax.random.normal(jax.random.fold_in(_gk, 1), (6250, 128), jnp.float32)
        src = jax.random.randint(jax.random.fold_in(_gk, 2), (100000,), 0, 6250, jnp.int32)
        dst = jax.random.randint(jax.random.fold_in(_gk, 3), (100000,), 0, 6250, jnp.int32)
        _o = jnp.argsort(dst, stable=True)
        src = src[_o]
        dst = dst[_o]
        edge_attr_16 = 0.000254156 + 0.999948 * jax.random.normal(jax.random.fold_in(_gk, 11), (100000, 16), jnp.float32)
        return (x, src, dst, edge_attr_16)
    x, src, dst, edge_attr_16 = _rec_inputs()

    def _L0_gnn_setup():
        import jax, jax.numpy as jnp
        import numpy as np
        N = 6250
        IN_DIM = 128
        HIDDEN = 128
        EDGE_DIM = 16
        E = 100000

        def _linear_init(key, fan_in, fan_out):
            kw, kb = jax.random.split(key)
            bound = 1.0 / np.sqrt(fan_in)
            W = jax.random.uniform(kw, (fan_in, fan_out), minval=-bound, maxval=bound, dtype=jnp.float32)
            b = jax.random.uniform(kb, (fan_out,), minval=-bound, maxval=bound, dtype=jnp.float32)
            return (W, b)
        key = jax.random.key(seed)
        k = jax.random.split(key, 8)
        h = jax.random.normal(k[0], (N, IN_DIM), dtype=jnp.float32)
        edge_index = jax.random.randint(k[1], (2, E), 0, N, dtype=jnp.int64)
        edge_feat = jax.random.normal(k[2], (E, EDGE_DIM), dtype=jnp.float32)
        W1, b1 = _linear_init(k[3], 2 * IN_DIM + EDGE_DIM, HIDDEN)
        W2, b2 = _linear_init(k[4], HIDDEN, HIDDEN)
        W3, b3 = _linear_init(k[5], IN_DIM + HIDDEN, HIDDEN)
        W4, b4 = _linear_init(k[6], HIDDEN, HIDDEN)
        return {'h': h, 'edge_index': edge_index, 'edge_feat': edge_feat, 'W1': W1, 'b1': b1, 'W2': W2, 'b2': b2, 'W3': W3, 'b3': b3, 'W4': W4, 'b4': b4}
    _L0_gnn_all = _L0_gnn_setup()
    _L0_gnn_in = {k: v for k, v in _L0_gnn_all.items() if k in ('W1', 'b1', 'W2', 'b2', 'W3', 'b3', 'W4', 'b4')}
    del _L0_gnn_all

    def _L1_gnn_setup():
        import jax, jax.numpy as jnp
        import numpy as np
        N_NODES = 6250
        N_EDGES = 100000
        D = 128
        LN_EPS = 1e-05
        key = jax.random.key(seed)
        ks = jax.random.split(key, 8)
        h = jax.random.normal(ks[0], (N_NODES, D), dtype=jnp.float32)
        edge_index = jax.random.randint(ks[1], (2, N_EDGES), 0, N_NODES, dtype=jnp.int32)
        s = 1.0 / np.sqrt(D)
        W1 = jax.random.uniform(ks[2], (D, D), jnp.float32, -s, s)
        b1 = jax.random.uniform(ks[3], (D,), jnp.float32, -s, s)
        W2 = jax.random.uniform(ks[4], (D, D), jnp.float32, -s, s)
        b2 = jax.random.uniform(ks[5], (D,), jnp.float32, -s, s)
        eps = jnp.zeros((), jnp.float32)
        gamma = jnp.ones((D,), jnp.float32)
        beta = jnp.zeros((D,), jnp.float32)
        return {'h': h, 'edge_index': edge_index, 'eps': eps, 'W1': W1, 'b1': b1, 'W2': W2, 'b2': b2, 'gamma': gamma, 'beta': beta}
    _L1_gnn_all = _L1_gnn_setup()
    _L1_gnn_in = {k: v for k, v in _L1_gnn_all.items() if k in ('eps', 'W1', 'b1', 'W2', 'b2', 'gamma', 'beta')}
    del _L1_gnn_all
    return {'x': x, 'src': src, 'dst': dst, 'edge_attr_16': edge_attr_16, 'L0_gnn_W1': _L0_gnn_in['W1'], 'L0_gnn_b1': _L0_gnn_in['b1'], 'L0_gnn_W2': _L0_gnn_in['W2'], 'L0_gnn_b2': _L0_gnn_in['b2'], 'L0_gnn_W3': _L0_gnn_in['W3'], 'L0_gnn_b3': _L0_gnn_in['b3'], 'L0_gnn_W4': _L0_gnn_in['W4'], 'L0_gnn_b4': _L0_gnn_in['b4'], 'L1_gnn_eps': _L1_gnn_in['eps'], 'L1_gnn_W1': _L1_gnn_in['W1'], 'L1_gnn_b1': _L1_gnn_in['b1'], 'L1_gnn_W2': _L1_gnn_in['W2'], 'L1_gnn_b2': _L1_gnn_in['b2'], 'L1_gnn_gamma': _L1_gnn_in['gamma'], 'L1_gnn_beta': _L1_gnn_in['beta']}

def reference(x, src, dst, edge_attr_16, L0_gnn_W1, L0_gnn_b1, L0_gnn_W2, L0_gnn_b2, L0_gnn_W3, L0_gnn_b3, L0_gnn_W4, L0_gnn_b4, L1_gnn_eps, L1_gnn_W1, L1_gnn_b1, L1_gnn_W2, L1_gnn_b2, L1_gnn_gamma, L1_gnn_beta):
    import jax
    import jax.numpy as jnp

    def _L0_gnn_ref(h, edge_index, edge_feat, W1, b1, W2, b2, W3, b3, W4, b4):
        import jax, jax.numpy as jnp
        import numpy as np
        N = 6250
        IN_DIM = 128
        HIDDEN = 128
        EDGE_DIM = 16
        E = 100000

        def _linear_init(key, fan_in, fan_out):
            kw, kb = jax.random.split(key)
            bound = 1.0 / np.sqrt(fan_in)
            W = jax.random.uniform(kw, (fan_in, fan_out), minval=-bound, maxval=bound, dtype=jnp.float32)
            b = jax.random.uniform(kb, (fan_out,), minval=-bound, maxval=bound, dtype=jnp.float32)
            return (W, b)
        src, dst = (edge_index[0], edge_index[1])
        msg_input = jnp.concatenate([h[src], h[dst], edge_feat], axis=-1)
        messages = jax.nn.silu(msg_input @ W1 + b1) @ W2 + b2
        agg = jax.ops.segment_sum(messages, dst, num_segments=h.shape[0])
        upd_in = jnp.concatenate([h, agg], axis=-1)
        h_new = jax.nn.silu(upd_in @ W3 + b3) @ W4 + b4
        return h_new + h

    def _L1_gnn_ref(h, edge_index, eps, W1, b1, W2, b2, gamma, beta):
        import jax, jax.numpy as jnp
        import numpy as np
        N_NODES = 6250
        N_EDGES = 100000
        D = 128
        LN_EPS = 1e-05
        src, dst = (edge_index[0], edge_index[1])
        agg = jax.ops.segment_sum(h[src], dst, num_segments=h.shape[0])
        z = (1.0 + eps) * h + agg
        z = jax.nn.relu(z @ W1 + b1) @ W2 + b2
        r = z + h
        mu = jnp.mean(r, axis=-1, keepdims=True)
        var = jnp.mean((r - mu) ** 2, axis=-1, keepdims=True)
        ln = (r - mu) * jax.lax.rsqrt(var + LN_EPS) * gamma + beta
        return jax.nn.relu(ln)
    edge_index = jnp.stack([src, dst])
    x = _layernorm(x + _L0_gnn_ref(x, edge_index, edge_attr_16, L0_gnn_W1, L0_gnn_b1, L0_gnn_W2, L0_gnn_b2, L0_gnn_W3, L0_gnn_b3, L0_gnn_W4, L0_gnn_b4), axis=-1)
    x = _layernorm(x + _L1_gnn_ref(x, edge_index, L1_gnn_eps, L1_gnn_W1, L1_gnn_b1, L1_gnn_W2, L1_gnn_b2, L1_gnn_gamma, L1_gnn_beta), axis=-1)
    return x

_drawn_inputs = setup_inputs


def setup_inputs(seed=0):
    import zlib

    import numpy as np

    out = dict(_drawn_inputs(seed))
    spreads = {'L1_gnn_gamma': (1.0, 0.2), 'L1_gnn_beta': (0.0, 0.1)}
    factors = {'edge_attr_16': 4.448,
     'L0_gnn_b1': 2.826,
     'L0_gnn_b3': 5.784,
     'L1_gnn_b1': 7.785,
     'L1_gnn_b2': 2.846}
    for name, (base, spread) in spreads.items():
        noise = np.random.default_rng([zlib.crc32(name.encode()), seed]).standard_normal(out[name].shape)
        drawn = base * np.exp(spread * noise) if base else spread * noise
        out[name] = jnp.asarray(drawn.astype(out[name].dtype))
    for name, factor in factors.items():
        out[name] = (out[name] * factor).astype(out[name].dtype)
    return out
```

```python
from contextlib import ExitStack

import concourse.bass as bass
from concourse import mybir

ACT = mybir.ActivationFunctionType
ALU = mybir.AluOpType
AX_X = mybir.AxisListType.X
F32 = mybir.dt.float32
I32 = mybir.dt.int32
ds = bass.ds

P = 128
D = 128
FE = 16
CH = 4
GE = CH * P
W = 64
BT = 4
BN = BT * P
START = 4
PAD_DST = -1000.0
LN_EPS = 1e-5


def done(n):
    return n + 1 + START


def build(nc, x, src, dst, ef, W1, b1, W2, b2, W3, b3, W4, b4, eps, V1, c1, V2, c2, gamma, beta, out):
    N, E = x.shape[0], src.shape[0]
    NG = -(-E // GE)
    NPAIR = NG // 2
    IT = NPAIR // 2
    assert NG % 4 == 0 and N % P and NG > P
    NT = -(-N // P)
    NPAD = NT * P
    NB = NT // BT
    TAIL = NT - NB * BT
    assert TAIL == 1 and NB % 2 == 0
    LAST_ROWS = N - (NT - 1) * P
    LAST_E = E - (NG - 1) * GE
    LAST_P = LAST_E // CH
    assert LAST_E % CH == 0
    GT = NG - P

    A_d = nc.dram_tensor("src_term", (NPAD, D), F32).ap()
    B_d = nc.dram_tensor("dst_term", (NPAD, D), F32).ap()
    x1_d = nc.dram_tensor("layer1_input", (NPAD, D), F32).ap()

    with ExitStack() as ctx:
        def sb(name, shape, dt=F32):
            return ctx.enter_context(nc.sbuf_tensor(name, shape, dt))

        def sem(name):
            return ctx.enter_context(nc.semaphore(name))

        counters = {}

        def counter(name, engine):
            counters.setdefault(engine, []).append(sem(name))
            return counters[engine][-1]

        ident = sb("ident", [P, P])
        ones = sb("ones", [P, P])
        iota_w = sb("iota_w", [P, W])
        iota_p = sb("iota_p", [P, 1])
        mhalf = sb("mhalf", [P, BT])
        wab = sb("wab", [P, 2 * D])
        wef = sb("wef", [P, CH * D])
        w2 = sb("w2", [P, D])
        w2t = sb("w2t", [P, D])
        w3 = sb("w3", [P, 2, D])
        w23 = sb("w23", [P, D])
        cdeg = sb("cdeg", [P, D])
        w4 = sb("w4", [P, D])
        v1 = sb("v1", [P, D])
        v2 = sb("v2", [P, D])
        b1_bc = sb("b1_bc", [P, D])
        b4_bc = sb("b4_bc", [P, D])
        c2_bc = sb("c2_bc", [P, D])
        gamma_bc = sb("gamma_bc", [P, D])
        beta_bc = sb("beta_bc", [P, D])
        b2_col = sb("b2_col", [P, 1])
        b3_col = sb("b3_col", [P, 1])
        c1_col = sb("c1_col", [P, 1])
        one_eps = sb("one_eps", [P, 1])
        src_rows = sb("src_rows", [P, 2, GE], I32)
        dst_rows = sb("dst_rows", [P, 2, GE], I32)
        rows_f = sb("rows_f", [P, 2, GE])
        src_col = sb("src_col", [P, (NG + 4) * CH], I32)
        dst_col = sb("dst_col", [P, NG * CH])
        dst_rel = sb("dst_rel", [P, NG * CH])
        lo = sb("lo", [P, 2])
        base_diag = sb("base_diag", [P, 2, P])
        base_bc = sb("base_bc", [P, 2 * P])
        base_i = sb("base_i", [P, 2 * P], I32)
        node_col = sb("node_col", [P, NPAIR])
        xT = sb("xT", [P, NPAD])
        S = sb("S", [P, 2, NPAD])
        T = sb("T", [P, NPAD])
        xs = sb("xs", [P, 2, BT, D])
        xTs = sb("xTs", [P, 2, BN])
        As = sb("As", [P, 2, BT, D])
        Bs = sb("Bs", [P, 2, BT, D])
        idx = sb("idx", [P, 2, 2 * CH], I32)
        gath = sb("gath", [P, 4, CH * D])
        dst_bc = sb("dst_bc", [P, 2, GE], I32)
        bwin = sb("bwin", [P, 2, D])
        ef_s = sb("ef_s", [P, 2, 2 * CH * FE])
        ef_T = sb("ef_T", [P, 2, P])
        oh = sb("oh", [P, 2, CH, W])
        ohT = sb("ohT", [P, 2, GE])
        pre = sb("pre", [P, 2, CH * D])
        msg = sb("msg", [P, 2, CH * D])
        hid = sb("hid", [P, 2, BN])
        v = sb("v", [P, 2, BT, D])
        st = sb("st", [P, 2, BT, 6])
        mv = sb("mv", [P, 2, BT, 2])
        ve = sb("ve", [P, 2, BT])
        rstd = sb("rstd", [P, 2, BT])
        nrm = sb("nrm", [P, 2, BT, D])

        bank = [ctx.enter_context(nc.psum_tensor(f"bank{i}", [P, 512], F32)) for i in range(8)]

        wab_in = sem("wab_in")
        src_in = sem("src_in")
        dst_in = sem("dst_in")
        wef_in = sem("wef_in")
        w_in = sem("w_in")
        x_in = [sem(f"x_in{u}") for u in range(2)]
        A_out = [sem(f"A_out{u}") for u in range(2)]
        B_out = [sem(f"B_out{u}") for u in range(2)]
        gathered0 = [sem(f"gathered0_{s}") for s in range(4)]
        gathered1 = [sem(f"gathered1_{s}") for s in range(4)]
        dst_bc_in = [sem(f"dst_bc_in{u}") for u in range(2)]
        bwin_in = [sem(f"bwin_in{u}") for u in range(2)]
        ef_in = [sem(f"ef_in{u}") for u in range(2)]
        x2_in = [sem(f"x2_in{u}") for u in range(2)]
        x1_out = [sem(f"x1_out{u}") for u in range(2)]
        x1_in = [sem(f"x1_in{u}") for u in range(2)]
        y_out = [sem(f"y_out{u}") for u in range(2)]
        id_zero = sem("id_zero")
        consts = sem("consts")
        zeroed = sem("zeroed")
        wef_zero = sem("wef_zero")
        src_prep = sem("src_prep")
        src_turned = sem("src_turned")
        src_ready = sem("src_ready")
        dst_prep = sem("dst_prep")
        dst_turned = sem("dst_turned")
        dst_ready = sem("dst_ready")
        base_turned = sem("base_turned")
        base_ready = sem("base_ready")
        rel_ready = sem("rel_ready")
        w2_turned = sem("w2_turned")
        w2_ready = sem("w2_ready")
        w23_ps = sem("w23_ps")
        w23_ready = sem("w23_ready")
        x_turned = counter("x_turned", "pe")
        xTs_made = counter("xTs_made", "act")
        xT_kept = counter("xT_kept", "dve")
        ab_ps = counter("ab_ps", "pe")
        A_made = counter("A_made", "dve")
        B_made = counter("B_made", "act")
        staged0 = counter("staged0", "dve")
        ohT_made = counter("ohT_made", "dve")
        oh_made = counter("oh_made", "dve")
        ef_turned = counter("ef_turned", "pe")
        efT_made = counter("efT_made", "act")
        pre_ps = counter("pre_ps", "pe")
        pre_made = counter("pre_made", "dve")
        msg_made = counter("msg_made", "act")
        sums_ps = counter("sums_ps", "pe")
        sums_added = counter("sums_added", "dve")
        upd_ps = counter("upd_ps", "pe")
        hid_made = counter("hid_made", "act")
        hnew_ps = counter("hnew_ps", "pe")
        xb_made = counter("xb_made", "dve")
        v_made = counter("v_made", "dve")
        st_made = counter("st_made", "dve")
        mv_made = counter("mv_made", "dve")
        ve_made = counter("ve_made", "pool")
        rstd_made = counter("rstd_made", "pool")
        x1_made = counter("x1_made", "dve")
        x1_turned = counter("x1_turned", "pe")
        T_init = counter("T_init", "act")
        staged1 = counter("staged1", "dve")
        oh1_made = counter("oh1_made", "dve")
        agg_ps = counter("agg_ps", "pe")
        agg_added = counter("agg_added", "dve")
        z_ps = counter("z_ps", "pe")
        z_made = counter("z_made", "act")
        r_ps = counter("r_ps", "pe")
        rb_made = counter("rb_made", "dve")
        r_made = counter("r_made", "dve")
        rst_made = counter("rst_made", "dve")
        rmv_made = counter("rmv_made", "dve")
        rve_made = counter("rve_made", "pool")
        rrstd_made = counter("rrstd_made", "pool")
        rn_made = counter("rn_made", "dve")
        rg_made = counter("rg_made", "pool")
        rh_made = counter("rh_made", "pool")
        y_made = counter("y_made", "dve")
        yst_made = counter("yst_made", "dve")
        ymv_made = counter("ymv_made", "dve")
        yve_made = counter("yve_made", "pool")
        yrstd_made = counter("yrstd_made", "pool")
        o_made = counter("o_made", "dve")

        def start_counters(eng, name):
            for s in counters.get(name, []):
                eng.sem_inc(s, START)

        def blocks(eng, body, peeled=False):
            if peeled:
                for u in range(2):
                    body(u, u, 0, BT)
            with eng.Fori(int(peeled), NB // 2) as t:
                for u in range(2):
                    body(2 * t + u, u, t, BT)
            body(NB, 0, NB // 2, TAIL)

        def pairs(eng, body):
            with eng.Fori(0, IT) as t:
                for u in range(2):
                    body(2 * t + u, u, t)

        def cols(b, nt):
            return ds(b * BN, nt * P)

        SLOT_BLOCKS = [NB // 2 + 1, NB // 2]
        x_v = x[0:NB * BN, :].rearrange("(n t p) d -> p n t d", t=BT, p=P)
        A_v = A_d[0:NB * BN, :].rearrange("(n t p) d -> p n t d", t=BT, p=P)
        B_v = B_d[0:NB * BN, :].rearrange("(n t p) d -> p n t d", t=BT, p=P)
        x1_v = x1_d[0:NB * BN, :].rearrange("(n t p) d -> p n t d", t=BT, p=P)
        o_v = out[0:NB * BN, :].rearrange("(n t p) d -> p n t d", t=BT, p=P)

        def row(a):
            return a.rearrange("(a n) -> a n", a=1)

        def col(a):
            return a.rearrange("(n a) -> n a", a=1)

        block = ctx.enter_context(nc.Block())

        @block.sync
        def _(sp):
            start_counters(sp, "sp")

            def load_rows(rows, of, s):
                sp.dma_start(rows[:, 0, :], of[0:P * GE].rearrange("(g e) -> g e", e=GE)).then_inc(s, 16)
                sp.dma_start(rows[0:GT - 1, 1, :],
                             of[P * GE:(NG - 1) * GE].rearrange("(g e) -> g e", e=GE)).then_inc(s, 16)
                sp.dma_start(rows[GT - 1:GT, 1, 0:LAST_E], row(of[(NG - 1) * GE:E])).then_inc(s, 16)
                sp.dma_start(rows[GT - 1:GT, 1, LAST_E:GE], row(of[E - (GE - LAST_E):E])).then_inc(s, 16)

            load_rows(src_rows, src, src_in)
            sp.dma_start(wab[:, 0:D], W1[0:D, :]).then_inc(wab_in, 16)
            sp.dma_start(wab[:, D:2 * D], W1[D:2 * D, :]).then_inc(wab_in, 16)
            sp.dma_start(b1_bc[:, :], row(b1).to_broadcast([P, D])).then_inc(wab_in, 16)

            for u in range(2):
                sp.dma_start(xs[:, u, :, :], x_v[:, u, :, :]).then_inc(x_in[u], 16)
            load_rows(dst_rows, dst, dst_in)
            def store_A(b, u):
                sp.wait_ge(A_made, done(b))
                sp.dma_start(A_v[:, ds(b, 1), :, :].rearrange("p a t d -> p (a t) d"),
                             As[:, u, :, :]).then_inc(A_out[u], 16)

            with sp.Fori(0, NB // 2 - 1) as t:
                for u in range(2):
                    sp.wait_ge(x_turned, done(2 * t + u))
                    sp.dma_start(xs[:, u, :, :], x_v[:, ds(2 * t + (2 + u), 1), :, :]
                                 .rearrange("p a t d -> p (a t) d")).then_inc(x_in[u], 16)
                    store_A(2 * t + u, u)
            sp.wait_ge(x_turned, done(NB - 2))
            sp.dma_start(xs[0:LAST_ROWS, 0, 0, :], x[NB * BN:N, :]).then_inc(x_in[0], 16)
            store_A(NB - 2, 0)
            store_A(NB - 1, 1)
            sp.wait_ge(A_made, done(NB))
            sp.dma_start(A_d[NB * BN:NPAD, :], As[:, 0, 0, :]).then_inc(A_out[0], 16)

            sp.wait_ge(wef_zero, 1)
            for h in range(2):
                for j in range(CH):
                    r = h * W + j * FE
                    sp.dma_start(wef[r:r + FE, j * D:(j + 1) * D], W1[2 * D:2 * D + FE, :]).then_inc(wef_in, 16)

            sp.wait_ge(base_ready, 1)
            for u in range(2):
                sp.wait_ge(B_out[u], 16 * SLOT_BLOCKS[u])

            def load_pair(k, u, last):
                sp.wait_ge(ohT_made, done(k - 2))
                for h in range(2):
                    to = dst_bc[h * W:(h + 1) * W, u, :]
                    if last and h:
                        sp.dma_start(to[:, 0:LAST_E], row(dst[(NG - 1) * GE:E]).to_broadcast([W, LAST_E])) \
                            .then_inc(dst_bc_in[u], 16)
                        rest = GE - LAST_E
                        sp.dma_start(to[:, LAST_E:GE], row(dst[E - rest:E]).to_broadcast([W, rest])) \
                            .then_inc(dst_bc_in[u], 16)
                    else:
                        sp.dma_start(to, row(dst[ds((2 * k + h) * GE, GE)]).to_broadcast([W, GE])) \
                            .then_inc(dst_bc_in[u], 16)
                sp.wait_ge(pre_ps, done(2 * k - 3))
                for h in range(2):
                    at = sp.value_load(base_i[0:1, ds(2 * k + h, 1)], min_val=0, max_val=NPAD - W)
                    sp.dma_start(bwin[h * W:(h + 1) * W, u, :], B_d[ds(at, W), :]).then_inc(bwin_in[u], 16)
                sp.wait_ge(ef_turned, done(k - 2))
                to = ef_s[:, u, :].rearrange("p (h f) -> p h f", h=2)
                if last:
                    e0 = 2 * k * GE
                    sp.dma_start(to[:, 0, :], ef[e0:e0 + GE, :].rearrange("(p j) f -> p (j f)", j=CH)) \
                        .then_inc(ef_in[u], 16)
                    sp.dma_start(to[0:LAST_P, 1, :],
                                 ef[e0 + GE:E, :].rearrange("(p j) f -> p (j f)", j=CH)).then_inc(ef_in[u], 16)
                    sp.dma_start(to[LAST_P:P, 1, :],
                                 ef[0:GE - LAST_E, :].rearrange("(p j) f -> p (j f)", j=CH)) \
                        .then_inc(ef_in[u], 16)
                else:
                    sp.dma_start(to, ef[ds(2 * k * GE, 2 * GE), :].rearrange("(h p j) f -> p h (j f)", h=2, j=CH)) \
                        .then_inc(ef_in[u], 16)

            with sp.Fori(0, IT - 1) as t:
                for u in range(2):
                    load_pair(2 * t + u, u, False)
            for u in range(2):
                load_pair(NPAIR - 2 + u, u, u == 1)

            def node_blocks(load, loaded, made, store, stored):
                for u in range(2):
                    sp.dma_start(xs[:, u, :, :], load[:, u, :, :]).then_inc(loaded[u], 16)

                def swap(b, u):
                    sp.wait_ge(made, done(b))
                    sp.dma_start(store[:, ds(b, 1), :, :].rearrange("p a t d -> p (a t) d"),
                                 As[:, u, :, :]).then_inc(stored[u], 16)

                with sp.Fori(0, NB // 2 - 1) as t:
                    for u in range(2):
                        swap(2 * t + u, u)
                        sp.dma_start(xs[:, u, :, :], load[:, ds(2 * t + (2 + u), 1), :, :]
                                     .rearrange("p a t d -> p (a t) d")).then_inc(loaded[u], 16)
                swap(NB - 2, 0)
                tail = load.tensor[NB * BN:N, :]
                sp.dma_start(xs[0:LAST_ROWS, 0, 0, :], tail).then_inc(loaded[0], 16)
                swap(NB - 1, 1)
                sp.wait_ge(made, done(NB))
                sp.dma_start(store.tensor[NB * BN:N, :], As[0:LAST_ROWS, 0, 0, :]).then_inc(stored[0], 16)
                for u in range(2):
                    sp.wait_ge(stored[u], 16 * SLOT_BLOCKS[u])

            node_blocks(x_v, x2_in, x1_made, x1_v, x1_out)
            node_blocks(x1_v, x1_in, o_made, o_v, y_out)

        @block.gpsimd
        def _(pool):
            start_counters(pool, "pool")
            g = nc.gpsimd
            g.memset(ident[:, :], 0.0).then_inc(id_zero, 1)
            g.memset(ones[:, :], 1.0)
            g.memset(mhalf[:, :], -0.5)
            g.iota(iota_w[:, :], [[1, W]], base=0, channel_multiplier=0, allow_small_or_imprecise_dtypes=True)
            g.iota(iota_p[:, :], [[0, 1]], base=0, channel_multiplier=1, allow_small_or_imprecise_dtypes=True)
            g.memset(lo[:, :], 0.0)
            g.memset(src_col[:, NG * CH:], 0)
            g.memset(dst_col[:, (NG - 1) * CH:], PAD_DST)
            pool.wait_ge(id_zero, 1)
            g.affine_select(out=ident[:, :], in_=ident[:, :], compare_op=ALU.not_equal, fill=1.0, base=0,
                            pattern=[[-1, P]], channel_multiplier=1).then_inc(consts, 1)
            g.memset(cdeg[:, :], 0.0)
            g.memset(wef[:, :], 0.0).then_inc(wef_zero, 1)
            g.memset(S[:, :, :], 0.0).then_inc(zeroed, 1)

            for u in range(2):
                pool.wait_ge(A_out[u], 16 * SLOT_BLOCKS[u])

            def gather(table, staged, used, gathered, k, u):
                pool.wait_ge(staged, done(k))
                pool.nop(nofuse=True)
                for h in range(2):
                    pool.wait_ge(used, done(2 * k + (h - 4)))
                    pool.nop(nofuse=True)
                    s = 2 * u + h
                    for j in range(CH):
                        g.indirect_dma_start(
                            out=gath[:, s, j * D:(j + 1) * D], out_offset=None, in_=table[0:N, :],
                            in_offset=bass.IndirectOffsetOnAxis(ap=idx[:, u, h * CH + j:h * CH + j + 1], axis=0),
                        ).then_inc(gathered[s], 16)

            pairs(pool, lambda k, u, t: gather(A_d, staged0, pre_made, gathered0, k, u))

            def inv_std(b, u, nt, stats, plus_eps, made):
                pool.wait_ge(stats, done(b))
                pool.nop(nofuse=True)
                g.tensor_scalar_add(ve[:, u, 0:nt], mv[:, u, 0:nt, 1], LN_EPS).then_inc(plus_eps, 1)
                pool.wait_ge(plus_eps, done(b))
                g.tensor_tensor(rstd[:, u, 0:nt], ve[:, u, 0:nt], mhalf[:, 0:nt], ALU.pow).then_inc(made, 1)

            blocks(pool, lambda b, u, t, nt: inv_std(b, u, nt, mv_made, ve_made, rstd_made))

            for u in range(2):
                pool.wait_ge(x1_out[u], 16 * SLOT_BLOCKS[u])
            pairs(pool, lambda k, u, t: gather(x1_d, staged1, agg_ps, gathered1, k, u))

            def affine(b, u, t, nt):
                inv_std(b, u, nt, rmv_made, rve_made, rrstd_made)
                pool.wait_ge(rn_made, done(b))
                bc = [P, nt, D]
                g.tensor_tensor(nrm[:, u, 0:nt, :], nrm[:, u, 0:nt, :],
                                gamma_bc[:, :].unsqueeze(1).to_broadcast(bc), ALU.mult).then_inc(rg_made, 1)
                pool.wait_ge(rg_made, done(b))
                g.tensor_tensor(nrm[:, u, 0:nt, :], nrm[:, u, 0:nt, :],
                                beta_bc[:, :].unsqueeze(1).to_broadcast(bc), ALU.add).then_inc(rh_made, 1)
                inv_std(b, u, nt, ymv_made, yve_made, yrstd_made)

            blocks(pool, affine)

        @block.scalar
        def _(act):
            start_counters(act, "act")
            a = nc.scalar
            for to, of in ((w2[:, :], W2), (w3[:, :, :], W3.rearrange("(h k) n -> k h n", h=2)), (w4[:, :], W4),
                           (v1[:, :], V1), (v2[:, :], V2),
                           (b4_bc[:, :], row(b4).to_broadcast([P, D])), (c2_bc[:, :], row(c2).to_broadcast([P, D])),
                           (gamma_bc[:, :], row(gamma).to_broadcast([P, D])),
                           (beta_bc[:, :], row(beta).to_broadcast([P, D])),
                           (b2_col[:, :], col(b2)), (b3_col[:, :], col(b3)), (c1_col[:, :], col(c1)),
                           (one_eps[:, :], row(eps).to_broadcast([P, 1]))):
                act.dma_start(to, of).then_inc(w_in, 16)

            def terms(b, u, t, nt):
                act.wait_ge(x_turned, done(b))
                act.wait_ge(ab_ps, done(b - 2))
                act.wait_ge(xT_kept, done(b - 2))
                a.copy(xTs[:, u, 0:nt * P], bank[u][:, 0:nt * P]).then_inc(xTs_made, 1)
                act.wait_ge(A_made, done(b))
                if not (isinstance(t, int) and t == 0):
                    act.wait_ge(B_out[u], 16 * t)
                for q in range(-(-nt // 2)):
                    n = min(2, nt - 2 * q)
                    last = a.copy(Bs[:, u, 2 * q:2 * q + n, :],
                                  bank[2 + 2 * u + q][:, :].rearrange("p (t d) -> p t d", t=2)[:, 0:n, D:])
                last.then_inc(B_made, 1)
                act.wait_ge(B_made, done(b))
                if nt == BT:
                    store = B_v[:, ds(b, 1), :, :].rearrange("p a t d -> p (a t) d")
                    act.dma_start(store, Bs[:, u, :, :]).then_inc(B_out[u], 16)
                else:
                    act.dma_start(B_d[NB * BN:NPAD, :], Bs[:, u, 0, :]).then_inc(B_out[u], 16)

            blocks(act, terms, peeled=True)

            def messages(k, u, t):
                act.wait_ge(ef_turned, done(k))
                act.wait_ge(pre_ps, done(2 * k - 3))
                a.copy(ef_T[:, u, :], bank[4][:, 0:P]).then_inc(efT_made, 1)
                for h in range(2):
                    g = 2 * k + h
                    act.wait_ge(pre_made, done(g))
                    act.wait_ge(sums_ps, done(g - 2))
                    a.activation(msg[:, h, :], pre[:, h, :], ACT.Silu).then_inc(msg_made, 1)

            pairs(act, messages)

            act.wait_ge(w_in, 16 * 13)

            def update(b, u, t, nt):
                act.wait_ge(upd_ps, done(b))
                act.wait_ge(hnew_ps, done(b - 2))
                a.activation(hid[:, u, 0:nt * P], bank[u][:, 0:nt * P], ACT.Silu,
                             bias=b3_col[:, :]).then_inc(hid_made, 1)
                act.wait_ge(x1_turned, done(b))
                a.activation(T[:, cols(b, nt)], bank[4 + u][:, 0:nt * P], ACT.Copy,
                             scale=one_eps[:, :]).then_inc(T_init, 1)

            act.wait_ge(dst_ready, 3)
            blocks(act, update)

            def hidden(b, u, t, nt):
                act.wait_ge(z_ps, done(b))
                act.wait_ge(r_ps, done(b - 2))
                a.activation(hid[:, u, 0:nt * P], bank[u][:, 0:nt * P], ACT.Relu,
                             bias=c1_col[:, :]).then_inc(z_made, 1)

            blocks(act, hidden)

        @block.tensor
        def _(pe):
            start_counters(pe, "pe")
            mm = nc.tensor.matmul

            def turn_rows(prep, turned):
                pe.wait_ge(prep, 1)
                for q, n in ((0, P), (1, GT)):
                    for j in range(CH):
                        last = nc.tensor.transpose(
                            bank[6 + q][:, j * P:j * P + n],
                            rows_f[0:n, q, :].rearrange("g (p j) -> g j p", j=CH)[:, j, :], ident[0:n, 0:n])
                last.then_inc(turned, 1)

            pe.wait_ge(consts, 1)
            turn_rows(src_prep, src_turned)
            pe.wait_ge(wab_in, 16 * 3)

            def terms(b, u, t, nt):
                pe.wait_ge(x_in[u], 16 * (t + 1))
                pe.wait_ge(xTs_made, done(b - 2))
                for j in range(nt):
                    last = nc.tensor.transpose(bank[u][:, j * P:(j + 1) * P], xs[:, u, j, :], ident[:, :])
                last.then_inc(x_turned, 1)
                pe.wait_ge(xTs_made, done(b))
                pe.wait_ge(B_made, done(b - 2))
                for j in range(nt):
                    last = mm(bank[2 + 2 * u + j // 2][:, (j % 2) * 2 * D:(j % 2 + 1) * 2 * D],
                              xTs[:, u, j * P:(j + 1) * P], wab[:, :], start=True, stop=True)
                last.then_inc(ab_ps, 1)

            blocks(pe, terms)

            pe.wait_ge(src_ready, 1)
            turn_rows(dst_prep, dst_turned)
            pe.wait_ge(dst_ready, 1)
            mm(bank[0][:, 0:2 * P], ones[:, :], base_diag[:, :, :].rearrange("p q g -> p (q g)"),
               start=True, stop=True).then_inc(base_turned, 1)
            pe.wait_ge(w_in, 16 * 13)
            nc.tensor.transpose(bank[1][:, 0:D], w2[:, :], ident[:, :]).then_inc(w2_turned, 1)
            pe.wait_ge(w2_ready, 1)
            mm(bank[1][:, D:2 * D], w2t[:, :], w3[:, 1, :], start=True, stop=True)
            mm(bank[1][0:1, 2 * D:3 * D], b2_col[:, :], w3[:, 1, :], start=True, stop=True).then_inc(w23_ps, 1)
            pe.wait_ge(w23_ready, 1)
            pe.wait_ge(B_made, done(NB))
            pe.wait_ge(wef_in, 16 * 2 * CH)

            def edges0(k, u, ef_count, dst_count):
                pe.wait_ge(ef_in[u], ef_count)
                pe.wait_ge(efT_made, done(k - 1))
                nc.tensor.transpose(bank[4][:, 0:P], ef_s[:, u, :], ident[:, :]).then_inc(ef_turned, 1)
                pe.wait_ge(efT_made, done(k))
                pe.wait_ge(bwin_in[u], dst_count)
                pe.wait_ge(ohT_made, done(k))
                for h in range(2):
                    g = 2 * k + h
                    r = slice(h * W, (h + 1) * W)
                    pe.wait_ge(pre_made, done(g - 2))
                    mm(bank[h][:, :], ef_T[r, u, :], wef[r, :], start=True, stop=False)
                    ohj = ohT[r, u, :].rearrange("n (p j) -> n j p", j=CH)
                    for j in range(CH):
                        last = mm(bank[h][:, j * D:(j + 1) * D], ohj[:, j, :], bwin[r, u, :],
                                  start=False, stop=j == CH - 1)
                    last.then_inc(pre_ps, 1)
                for h in range(2):
                    g = 2 * k + h
                    pe.wait_ge(msg_made, done(g))
                    pe.wait_ge(sums_added, done(g - 2))
                    for lhs, a0 in ((None, 0), (ones, 1)):
                        for j in range(CH):
                            w = ones[:, :] if lhs is ones else msg[:, h, j * D:(j + 1) * D]
                            last = mm(bank[2 + h][:, a0 * W:(a0 + 1) * W], w, oh[:, h, j, :],
                                      start=j == 0, stop=j == CH - 1)
                    last.then_inc(sums_ps, 1)

            with pe.Fori(0, IT - 1) as t:
                for u in range(2):
                    edges0(2 * t + u, u, 16 * (t + 1), 32 * (t + 1))
            edges0(NPAIR - 2, 0, 16 * IT, 32 * IT)
            edges0(NPAIR - 1, 1, 16 * (IT + 2), 32 * IT)

            pe.wait_ge(sums_added, done(NG - 1))
            pe.wait_ge(xT_kept, done(NB))

            def update(b, u, t, nt):
                n = nt * P
                pe.wait_ge(hid_made, done(b - 2))
                mm(bank[u][:, 0:n], w3[:, 0, :], xT[:, cols(b, nt)], start=True, stop=False)
                mm(bank[u][:, 0:n], w23[:, :], S[:, 0, cols(b, nt)], start=False, stop=False)
                mm(bank[u][:, 0:n], cdeg[:, :], S[:, 1, cols(b, nt)], start=False, stop=True).then_inc(upd_ps, 1)
                pe.wait_ge(hid_made, done(b))
                pe.wait_ge(v_made, done(b - 2))
                for j in range(nt):
                    last = mm(bank[2 + u][:, j * D:(j + 1) * D], hid[:, u, j * P:(j + 1) * P], w4[:, :],
                              start=True, stop=True)
                last.then_inc(hnew_ps, 1)
                pe.wait_ge(x1_made, done(b))
                pe.wait_ge(T_init, done(b - 2))
                for j in range(nt):
                    last = nc.tensor.transpose(bank[4 + u][:, j * P:(j + 1) * P], As[:, u, j, :], ident[:, :])
                last.then_inc(x1_turned, 1)

            blocks(pe, update)

            def edges1(k, u, t):
                for h in range(2):
                    g = 2 * k + h
                    s = 2 * u + h
                    pe.wait_ge(gathered1[s], 16 * CH * (t + 1))
                    pe.wait_ge(oh1_made, done(g))
                    pe.wait_ge(agg_added, done(g - 2))
                    for j in range(CH):
                        last = mm(bank[2 + h][:, 0:W], gath[:, s, j * D:(j + 1) * D], oh[:, h, j, :],
                                  start=j == 0, stop=j == CH - 1)
                    last.then_inc(agg_ps, 1)

            pe.wait_ge(v_made, done(NB))
            pairs(pe, edges1)

            pe.wait_ge(agg_added, done(NG - 1))

            def layer1(b, u, t, nt):
                n = nt * P
                pe.wait_ge(z_made, done(b - 2))
                mm(bank[u][:, 0:n], v1[:, :], T[:, cols(b, nt)], start=True, stop=True).then_inc(z_ps, 1)
                pe.wait_ge(z_made, done(b))
                pe.wait_ge(r_made, done(b - 2))
                for j in range(nt):
                    last = mm(bank[4 + u][:, j * D:(j + 1) * D], hid[:, u, j * P:(j + 1) * P], v2[:, :],
                              start=True, stop=True)
                last.then_inc(r_ps, 1)

            pe.wait_ge(T_init, done(NB))
            blocks(pe, layer1)

        @block.vector
        def _(dve):
            start_counters(dve, "dve")
            ve_ = nc.vector

            def cols_of(q, col, made):
                g0, n = (0, P) if q == 0 else (P, GT - 1)
                ps = bank[6 + q][:, :].rearrange("p (j g) -> p g j", j=CH)
                ve_.tensor_copy(col[:, g0 * CH:(g0 + n) * CH].rearrange("p (g j) -> p g j", j=CH), ps[:, 0:n, :])
                if q:
                    last_p = LAST_P if col is dst_col else P
                    return ve_.tensor_copy(col[0:last_p, (NG - 1) * CH:NG * CH], ps[0:last_p, n, :])

            def to_float(rows, landed, made):
                dve.wait_ge(landed, 16 * 4)
                ve_.tensor_copy(rows_f[:, 0, :], rows[:, 0, :])
                ve_.tensor_copy(rows_f[0:GT, 1, :], rows[0:GT, 1, :]).then_inc(made, 1)

            to_float(src_rows, src_in, src_prep)
            dve.wait_ge(consts, 1)
            dve.wait_ge(src_turned, 1)
            cols_of(0, src_col, None)
            cols_of(1, src_col, None).then_inc(src_ready, 1)

            dve.wait_ge(wab_in, 16 * 3)

            def terms(b, u, t, nt):
                dve.wait_ge(xTs_made, done(b))
                ve_.tensor_copy(xT[:, cols(b, nt)], xTs[:, u, 0:nt * P]).then_inc(xT_kept, 1)
                dve.wait_ge(ab_ps, done(b))
                if not (isinstance(t, int) and t == 0):
                    dve.wait_ge(A_out[u], 16 * t)
                for q in range(-(-nt // 2)):
                    n = min(2, nt - 2 * q)
                    last = ve_.tensor_tensor(
                        As[:, u, 2 * q:2 * q + n, :],
                        bank[2 + 2 * u + q][:, :].rearrange("p (t d) -> p t d", t=2)[:, 0:n, 0:D],
                        b1_bc[:, :].unsqueeze(1).to_broadcast([P, n, D]), ALU.add)
                last.then_inc(A_made, 1)

            blocks(dve, terms, peeled=True)

            def stage(k, u, staged):
                ve_.tensor_copy(idx[:, u, :], src_col[:, ds(k * (2 * CH), 2 * CH)]).then_inc(staged, 1)

            dve.wait_ge(src_ready, 1)
            for u in range(2):
                stage(u, u, staged0)

            dve.wait_ge(src_turned, 1)
            to_float(dst_rows, dst_in, dst_prep)
            dve.wait_ge(dst_prep, 1)
            dve.wait_ge(consts, 1)
            ve_.tensor_reduce(lo[:, 0:1], rows_f[:, 0, :], AX_X, ALU.min)
            ve_.tensor_reduce(lo[0:GT, 1:2], rows_f[0:GT, 1, :], AX_X, ALU.min).then_inc(rel_ready, 1)
            dve.wait_ge(rel_ready, 1)
            for q in range(2):
                last = ve_.tensor_scalar(base_diag[:, q, :], ident[:, :], lo[:, q:q + 1], float(NPAD - W),
                                         ALU.mult, ALU.min)
            last.then_inc(dst_ready, 1)
            dve.wait_ge(dst_turned, 1)
            cols_of(0, dst_col, None)
            cols_of(1, dst_col, None).then_inc(dst_ready, 1)
            dve.wait_ge(w_in, 16 * 13)
            ve_.tensor_scalar_add(one_eps[:, :], one_eps[:, :], 1.0).then_inc(dst_ready, 1)
            dve.wait_ge(base_turned, 1)
            ve_.tensor_copy(base_bc[:, :], bank[0][:, 0:2 * P])
            ve_.tensor_copy(base_i[:, :], bank[0][:, 0:2 * P]).then_inc(base_ready, 1)
            dve.wait_ge(base_ready, 1)
            dve.wait_ge(dst_ready, 3)
            ve_.tensor_tensor(dst_rel[:, :].rearrange("p (g j) -> p g j", j=CH),
                              dst_col[:, :].rearrange("p (g j) -> p g j", j=CH),
                              base_bc[:, 0:NG].unsqueeze(2).to_broadcast([P, NG, CH]), ALU.subtract)
            by_pair = base_bc[:, 0:NG].rearrange("p (k h) -> p k h", h=2)
            for h in range(2):
                r = slice(h * W, (h + 1) * W)
                last = ve_.tensor_scalar(node_col[r, :], by_pair[r, :, h], iota_p[r, :], float(-h * W),
                                         ALU.add, ALU.add)
            last.then_inc(rel_ready, 1)
            dve.wait_ge(w2_turned, 1)
            ve_.tensor_copy(w2t[:, :], bank[1][:, 0:D]).then_inc(w2_ready, 1)
            dve.wait_ge(w23_ps, 1)
            ve_.tensor_copy(w23[:, :], bank[1][:, D:2 * D])
            dve.wait_ge(wef_zero, 1)
            ve_.tensor_copy(cdeg[0:1, :], bank[1][0:1, 2 * D:3 * D]).then_inc(w23_ready, 1)
            dve.wait_ge(rel_ready, 2)
            dve.wait_ge(zeroed, 1)

            def one_hot(g, h, read, made):
                dve.wait_ge(read, done(g - 2))
                ve_.tensor_tensor(oh[:, h, :, :], iota_w[:, :].unsqueeze(1).to_broadcast([P, CH, W]),
                                  dst_rel[:, ds(g * CH, CH)].unsqueeze(2).to_broadcast([P, CH, W]),
                                  ALU.is_equal).then_inc(made, 1)

            def edges0(k, u, t, dst_count):
                dve.wait_ge(dst_bc_in[u], dst_count)
                dve.wait_ge(pre_ps, done(2 * k - 3))
                ve_.tensor_scalar(ohT[:, u, :], dst_bc[:, u, :], node_col[:, ds(k, 1)], None,
                                  ALU.is_equal).then_inc(ohT_made, 1)
                for h in range(2):
                    one_hot(2 * k + h, h, sums_ps, oh_made)
                for h in range(2):
                    g = 2 * k + h
                    s = 2 * u + h
                    dve.wait_ge(gathered0[s], 16 * CH * (t + 1))
                    dve.wait_ge(pre_ps, done(g))
                    dve.wait_ge(msg_made, done(g - 2))
                    ve_.tensor_tensor(pre[:, h, :], bank[h][:, :], gath[:, s, :], ALU.add).then_inc(pre_made, 1)
                stage(k + 2, u, staged0)
                for h in range(2):
                    g = 2 * k + h
                    at = dve.value_load(base_i[0:1, ds(g, 1)], min_val=0, max_val=NPAD - W)
                    dve.wait_ge(sums_ps, done(g))
                    dve.wait_ge(sums_added, done(g - 1))
                    ve_.tensor_tensor(S[:, :, ds(at, W)], S[:, :, ds(at, W)],
                                      bank[2 + h][:, 0:2 * W].rearrange("p (a w) -> p a w", a=2),
                                      ALU.add).then_inc(sums_added, 1)

            with dve.Fori(0, IT - 1) as t:
                for u in range(2):
                    edges0(2 * t + u, u, t, 32 * (t + 1))
            edges0(NPAIR - 2, 0, IT - 1, 32 * IT)
            edges0(NPAIR - 1, 1, IT - 1, 16 * (2 * IT + 1))

            dve.wait_ge(w_in, 16 * 13)

            def stats(b, nt, u, of, read, raw, made):
                dve.wait_ge(read, done(b))
                for j in range(nt):
                    last = ve_.bn_stats(st[:, u, j, :], of[:, u, j, :])
                last.then_inc(raw, 1)
                dve.wait_ge(raw, done(b))
                dve.nop(nofuse=True)
                for j in range(nt):
                    last = ve_.bn_aggr(mv[:, u, j, :], st[:, u, j, :])
                last.then_inc(made, 1)

            def normalise(b, nt, u, to, of, inv, made):
                dve.wait_ge(inv, done(b))
                for j in range(nt):
                    last = ve_.tensor_scalar(to[:, u, j, :], of[:, u, j, :], mv[:, u, j, 0:1], rstd[:, u, j:j + 1],
                                             ALU.subtract, ALU.mult)
                last.then_inc(made, 1)

            def update(b, u, t, nt):
                dve.wait_ge(x2_in[u], 16 * (t + 1))
                bc = b4_bc[:, :].unsqueeze(1).to_broadcast([P, nt, D])
                ve_.scalar_tensor_tensor(out=v[:, u, 0:nt, :], in0=xs[:, u, 0:nt, :], scalar=2.0, in1=bc,
                                         op0=ALU.mult, op1=ALU.add).then_inc(xb_made, 1)
                dve.wait_ge(xb_made, done(b))
                dve.wait_ge(hnew_ps, done(b))
                ve_.tensor_tensor(v[:, u, 0:nt, :], bank[2 + u][:, 0:nt * D].rearrange("p (t d) -> p t d", d=D),
                                  v[:, u, 0:nt, :], ALU.add).then_inc(v_made, 1)
                stats(b, nt, u, v, v_made, st_made, mv_made)
                if not (isinstance(t, int) and t == 0):
                    dve.wait_ge(x1_out[u], 16 * t)
                dve.wait_ge(x1_turned, done(b - 2))
                normalise(b, nt, u, As, v, rstd_made, x1_made)

            for u in range(2):
                dve.wait_ge(A_out[u], 16 * SLOT_BLOCKS[u])
            blocks(dve, update, peeled=True)

            for u in range(2):
                stage(u, u, staged1)
            dve.wait_ge(T_init, done(NB))

            def edges1(k, u, t):
                for h in range(2):
                    one_hot(2 * k + h, h, agg_ps, oh1_made)
                for h in range(2):
                    g = 2 * k + h
                    at = dve.value_load(base_i[0:1, ds(g, 1)], min_val=0, max_val=NPAD - W)
                    dve.wait_ge(agg_ps, done(g))
                    dve.wait_ge(agg_added, done(g - 1))
                    ve_.tensor_tensor(T[:, ds(at, W)], T[:, ds(at, W)], bank[2 + h][:, 0:W],
                                      ALU.add).then_inc(agg_added, 1)
                stage(k + 2, u, staged1)

            pairs(dve, edges1)

            def layer1(b, u, t, nt):
                dve.wait_ge(x1_in[u], 16 * (t + 1))
                bc = c2_bc[:, :].unsqueeze(1).to_broadcast([P, nt, D])
                ve_.tensor_tensor(v[:, u, 0:nt, :], xs[:, u, 0:nt, :], bc, ALU.add).then_inc(rb_made, 1)
                dve.wait_ge(rb_made, done(b))
                dve.wait_ge(r_ps, done(b))
                ve_.tensor_tensor(v[:, u, 0:nt, :], bank[4 + u][:, 0:nt * D].rearrange("p (t d) -> p t d", d=D),
                                  v[:, u, 0:nt, :], ALU.add).then_inc(r_made, 1)
                stats(b, nt, u, v, r_made, rst_made, rmv_made)
                normalise(b, nt, u, nrm, v, rrstd_made, rn_made)
                dve.wait_ge(rh_made, done(b))
                ve_.scalar_tensor_tensor(out=v[:, u, 0:nt, :], in0=nrm[:, u, 0:nt, :], scalar=0.0,
                                         in1=xs[:, u, 0:nt, :], op0=ALU.max, op1=ALU.add).then_inc(y_made, 1)
                stats(b, nt, u, v, y_made, yst_made, ymv_made)
                if not (isinstance(t, int) and t == 0):
                    dve.wait_ge(y_out[u], 16 * t)
                normalise(b, nt, u, As, v, yrstd_made, o_made)

            blocks(dve, layer1, peeled=True)


_INS = ['x', 'src', 'dst', 'edge_attr_16', 'L0_gnn_W1', 'L0_gnn_b1', 'L0_gnn_W2', 'L0_gnn_b2', 'L0_gnn_W3',
        'L0_gnn_b3', 'L0_gnn_W4', 'L0_gnn_b4', 'L1_gnn_eps', 'L1_gnn_W1', 'L1_gnn_b1', 'L1_gnn_W2', 'L1_gnn_b2',
        'L1_gnn_gamma', 'L1_gnn_beta']


def kernel(**inputs):
    import numpy as np
    import concourse.bacc as bacc
    from concourse.bass_utils import run_bass_kernel_spmd

    nc = bacc.Bacc("TRN2", target_bir_lowering=False, num_devices=1)
    arrays, args = {}, []
    for name in _INS:
        a = np.ascontiguousarray(inputs[name])
        if a.ndim == 0:
            a = a.reshape(1)
        arrays[f"in_{name}"] = a
        args.append(nc.dram_tensor(f"in_{name}", a.shape, mybir.dt.from_np(a.dtype), kind="ExternalInput").ap())
    out = nc.dram_tensor("out", tuple(inputs["x"].shape), F32, kind="ExternalOutput").ap()
    build(nc, *args, out)
    r = run_bass_kernel_spmd(nc, [arrays], core_ids=[0])
    return r.results[0]["out"]
```

```python
from contextlib import ExitStack

import concourse.bass as bass
from concourse import mybir

ACT = mybir.ActivationFunctionType
ALU = mybir.AluOpType
AX_X = mybir.AxisListType.X
F32 = mybir.dt.float32
I32 = mybir.dt.int32
ds = bass.ds

P = 128
D = 128
FE = 16
CH = 4
GE = CH * P
W = 64
PW = 2 * W
BT = 4
BN = BT * P
START = 4
PAD_DST = -1000.0
LN_EPS = 1e-5


def done(n):
    return n + 1 + START


def build(nc, x, src, dst, ef, W1, b1, W2, b2, W3, b3, W4, b4, eps, V1, c1, V2, c2, gamma, beta, out):
    N, E = x.shape[0], src.shape[0]
    NG = -(-E // GE)
    NPAIR = NG // 2
    IT = NPAIR // 2
    assert NG % 4 == 0 and N % P and NG > P
    NT = -(-N // P)
    NPAD = NT * P
    NB = NT // BT
    TAIL = NT - NB * BT
    assert TAIL == 1 and NB % 2 == 0
    LAST_ROWS = N - (NT - 1) * P
    LAST_E = E - (NG - 1) * GE
    LAST_P = LAST_E // CH
    assert LAST_E % CH == 0
    GT = NG - P

    A_d = nc.dram_tensor("src_term", (NPAD, D), F32).ap()
    B_d = nc.dram_tensor("dst_term", (NPAD, D), F32).ap()
    x1_d = nc.dram_tensor("layer1_input", (NPAD, D), F32).ap()

    with ExitStack() as ctx:
        def sb(name, shape, dt=F32):
            return ctx.enter_context(nc.sbuf_tensor(name, shape, dt))

        def sem(name):
            return ctx.enter_context(nc.semaphore(name))

        counters = {}

        def counter(name, engine):
            counters.setdefault(engine, []).append(sem(name))
            return counters[engine][-1]

        ident = sb("ident", [P, P])
        ones = sb("ones", [P, P])
        iota_w = sb("iota_w", [P, PW])
        iota_p = sb("iota_p", [P, 1])
        mhalf = sb("mhalf", [P, BT])
        wab = sb("wab", [P, 2 * D])
        w2 = sb("w2", [P, D])
        w2t = sb("w2t", [P, D])
        w3 = sb("w3", [P, 2, D])
        w23 = sb("w23", [P, D])
        cdeg = sb("cdeg", [P, D])
        w4 = sb("w4", [P, D])
        v1 = sb("v1", [P, D])
        v2 = sb("v2", [P, D])
        b1_bc = sb("b1_bc", [P, D])
        b4_bc = sb("b4_bc", [P, D])
        c2_bc = sb("c2_bc", [P, D])
        gamma_bc = sb("gamma_bc", [P, D])
        beta_bc = sb("beta_bc", [P, D])
        b2_col = sb("b2_col", [P, 1])
        b3_col = sb("b3_col", [P, 1])
        c1_col = sb("c1_col", [P, 1])
        one_eps = sb("one_eps", [P, 1])
        src_rows = sb("src_rows", [P, 2, GE], I32)
        dst_rows = sb("dst_rows", [P, 2, GE], I32)
        rows_f = sb("rows_f", [P, 2, GE])
        src_col = sb("src_col", [P, (NG + 4) * CH], I32)
        dst_col = sb("dst_col", [P, NG * CH])
        dst_rel = sb("dst_rel", [P, NG * CH])
        lo = sb("lo", [P, 2])
        base_diag = sb("base_diag", [P, 2, P])
        base_bc = sb("base_bc", [P, 2 * P])
        pair_bc = sb("pair_bc", [P, NPAIR])
        no_dst = sb("no_dst", [W, GE - LAST_E], I32)
        bases = sb("bases", [1, NPAIR, 4], I32)
        node_col = sb("node_col", [P, NPAIR])
        xT = sb("xT", [P, NPAD])
        S = sb("S", [P, NPAD])
        T = sb("T", [P, NPAD])
        xs = sb("xs", [P, 2, BT, D])
        xr = sb("xr", [P, 2, BT, D])
        xTs = sb("xTs", [P, 2, BN])
        As = sb("As", [P, 2, BT, D])
        Bs = sb("Bs", [P, 2, BT, D])
        idx = sb("idx", [P, 2, 2 * CH], I32)
        gath = sb("gath", [P, 4, CH * D])
        dst_bc = sb("dst_bc", [P, 2, GE], I32)
        terms_l = sb("terms_l", [P, 2, 2, CH, P])
        terms_r = sb("terms_r", [P, 2, 2, CH, D])
        deg_col = sb("deg_col", [P, 2])
        ef_s = sb("ef_s", [P, 2, 2 * CH * FE])
        oh = sb("oh", [P, 2, 2 * CH, PW])
        pre = sb("pre", [P, 2, CH * D])
        msg = sb("msg", [P, 4, CH * D])
        hid = sb("hid", [P, 2, BN])
        v = sb("v", [P, 2, BT, D])
        y = sb("y", [P, 2, BT, D])
        st = sb("st", [P, 2, 2, BT, 6])
        mv = sb("mv", [P, 2, 2, BT, 2])
        ve = sb("ve", [P, 2, 2, BT])
        rstd = sb("rstd", [P, 2, 2, BT])
        nrm = sb("nrm", [P, 2, BT, D])

        bank = [ctx.enter_context(nc.psum_tensor(f"bank{i}", [P, 512], F32)) for i in range(8)]

        wab_in = sem("wab_in")
        src_in = sem("src_in")
        dst_in = sem("dst_in")
        wef_in = sem("wef_in")
        w_in = sem("w_in")
        x_in = [sem(f"x_in{u}") for u in range(2)]
        A_out = [sem(f"A_out{u}") for u in range(2)]
        B_out = [sem(f"B_out{u}") for u in range(2)]
        gathered0 = [sem(f"gathered0_{s}") for s in range(4)]
        gathered1 = [sem(f"gathered1_{s}") for s in range(4)]
        dst_bc_in = [sem(f"dst_bc_in{u}") for u in range(2)]
        bwin_in = [sem(f"bwin_in{u}") for u in range(2)]
        ef_in = [sem(f"ef_in{u}") for u in range(2)]
        x2_in = [sem(f"x2_in{u}") for u in range(2)]
        x1_out = [sem(f"x1_out{u}") for u in range(2)]
        x1_in = [sem(f"x1_in{u}") for u in range(2)]
        xr_in = [sem(f"xr_in{u}") for u in range(2)]
        y_out = [sem(f"y_out{u}") for u in range(2)]
        id_zero = sem("id_zero")
        consts = sem("consts")
        zeroed = sem("zeroed")
        wef_zero = sem("wef_zero")
        src_prep = sem("src_prep")
        src_turned = sem("src_turned")
        src_ready = sem("src_ready")
        dst_prep = sem("dst_prep")
        dst_turned = sem("dst_turned")
        dst_ready = sem("dst_ready")
        base_turned = sem("base_turned")
        base_ready = sem("base_ready")
        rel_ready = sem("rel_ready")
        w2_turned = sem("w2_turned")
        w2_ready = sem("w2_ready")
        w23_ps = sem("w23_ps")
        w23_ready = sem("w23_ready")
        x_turned = counter("x_turned", "pe")
        xTs_made = counter("xTs_made", "act")
        xT_kept = counter("xT_kept", "dve")
        ab_ps = counter("ab_ps", "pe")
        A_made = counter("A_made", "dve")
        B_made = counter("B_made", "act")
        staged0 = counter("staged0", "dve")
        ohT_made = counter("ohT_made", "dve")
        oh_made = counter("oh_made", "dve")
        ef_turned = counter("ef_turned", "pe")
        efT_made = counter("efT_made", "act")
        pre_ps = counter("pre_ps", "pe")
        pre_made = counter("pre_made", "dve")
        msg_made = counter("msg_made", "act")
        sums_ps = counter("sums_ps", "pe")
        deg_added = counter("deg_added", "dve")
        sums_added = counter("sums_added", "dve")
        upd_ps = counter("upd_ps", "pe")
        hid_made = counter("hid_made", "act")
        hnew_ps = counter("hnew_ps", "pe")
        xb_made = counter("xb_made", "dve")
        v_made = counter("v_made", "dve")
        st_made = counter("st_made", "dve")
        mv_made = counter("mv_made", "dve")
        ve_made = counter("ve_made", "pool")
        rstd_made = counter("rstd_made", "pool")
        x1_made = counter("x1_made", "dve")
        x1_turned = counter("x1_turned", "pe")
        T_init = counter("T_init", "act")
        staged1 = counter("staged1", "dve")
        oh1_made = counter("oh1_made", "dve")
        agg_ps = counter("agg_ps", "pe")
        agg_added = counter("agg_added", "dve")
        z_ps = counter("z_ps", "pe")
        z_made = counter("z_made", "act")
        r_ps = counter("r_ps", "pe")
        rb_made = counter("rb_made", "dve")
        r_made = counter("r_made", "dve")
        rst_made = counter("rst_made", "dve")
        rmv_made = counter("rmv_made", "dve")
        rve_made = counter("rve_made", "pool")
        rrstd_made = counter("rrstd_made", "pool")
        rn_made = counter("rn_made", "dve")
        rg_made = counter("rg_made", "pool")
        rh_made = counter("rh_made", "pool")
        y_made = counter("y_made", "dve")
        yst_made = counter("yst_made", "dve")
        ymv_made = counter("ymv_made", "dve")
        yve_made = counter("yve_made", "pool")
        yrstd_made = counter("yrstd_made", "pool")
        o_made = counter("o_made", "dve")

        def start_counters(eng, name):
            for s in counters.get(name, []):
                eng.sem_inc(s, START)

        def skewed(eng, items, stages, loop_to):
            reach = max(lag for lag, _ in stages)

            def step(s, parity, half):
                for lag, body in stages:
                    slot = (parity - lag) % 2
                    if isinstance(s, int):
                        if 0 <= s - lag < items:
                            body(s - lag, slot, (s - lag) // 2)
                    else:
                        body(2 * half + (parity - lag), slot, half + (parity - lag - slot) // 2)

            first = 2 + reach + reach % 2
            for s in range(first):
                step(s, s % 2, None)
            with eng.Fori(first // 2, loop_to // 2) as half:
                for parity in range(2):
                    step(None, parity, half)
            for s in range(loop_to, items + reach):
                step(s, s % 2, None)

        def blocks(eng, *stages):
            def sized(body):
                return lambda b, u, t: body(b, u, t, TAIL if isinstance(b, int) and b == NB else BT)
            skewed(eng, NB + 1, [(lag, sized(body)) for lag, body in stages], NB)

        def pairs(eng, *stages):
            skewed(eng, NPAIR, stages, NPAIR - 2)

        def is_last(k):
            return isinstance(k, int) and k == NPAIR - 1

        def again(t):
            return not (isinstance(t, int) and t == 0)

        def cols(b, nt):
            return ds(b * BN, nt * P)

        SLOT_BLOCKS = [NB // 2 + 1, NB // 2]
        def row(a):
            return a.rearrange("(a n) -> a n", a=1)

        def col(a):
            return a.rearrange("(n a) -> n a", a=1)

        block = ctx.enter_context(nc.Block())

        @block.sync
        def _(sp):
            start_counters(sp, "sp")

            def load_rows(rows, of, s):
                sp.dma_start(rows[:, 0, :], of[0:P * GE].rearrange("(g e) -> g e", e=GE)).then_inc(s, 16)
                sp.dma_start(rows[0:GT - 1, 1, :],
                             of[P * GE:(NG - 1) * GE].rearrange("(g e) -> g e", e=GE)).then_inc(s, 16)
                sp.dma_start(rows[GT - 1:GT, 1, 0:LAST_E], row(of[(NG - 1) * GE:E])).then_inc(s, 16)
                sp.dma_start(rows[GT - 1:GT, 1, LAST_E:GE], row(of[E - (GE - LAST_E):E])).then_inc(s, 16)

            load_rows(src_rows, src, src_in)
            sp.dma_start(wab[:, 0:D], W1[0:D, :]).then_inc(wab_in, 16)
            sp.dma_start(wab[:, D:2 * D], W1[D:2 * D, :]).then_inc(wab_in, 16)
            sp.dma_start(b1_bc[:, :], row(b1).to_broadcast([P, D])).then_inc(wab_in, 16)

            load_rows(dst_rows, dst, dst_in)

            def load_block(of, to, loaded, read):
                def body(b, u, t, nt):
                    sp.wait_ge(read, done(b - 2))
                    if nt == BT:
                        sp.dma_start(to[:, u, :, :], of[0:NB * BN, :].rearrange("(n t p) d -> p n t d", t=BT, p=P)
                                     [:, ds(b, 1), :, :].rearrange("p a t d -> p (a t) d")).then_inc(loaded[u], 16)
                    else:
                        sp.dma_start(to[0:LAST_ROWS, u, 0, :], of[NB * BN:N, :]).then_inc(loaded[u], 16)
                return body

            def store_block(eng, of, to, stored, made, rows=LAST_ROWS):
                def body(b, u, t, nt):
                    eng.wait_ge(made, done(b))
                    if nt == BT:
                        eng.dma_start(to[0:NB * BN, :].rearrange("(n t p) d -> p n t d", t=BT, p=P)
                                      [:, ds(b, 1), :, :].rearrange("p a t d -> p (a t) d"),
                                      of[:, u, :, :]).then_inc(stored[u], 16)
                    else:
                        eng.dma_start(to[NB * BN:NB * BN + rows, :], of[0:rows, u, 0, :]).then_inc(stored[u], 16)
                return body

            def landed(stored):
                for u in range(2):
                    sp.wait_ge(stored[u], 16 * SLOT_BLOCKS[u])

            blocks(sp, (0, load_block(x, xs, x_in, x_turned)),
                   (2, store_block(sp, As, A_d, A_out, A_made, P)),
                   (2, store_block(sp, Bs, B_d, B_out, B_made, P)))

            sp.wait_ge(wef_zero, 1)
            for u in range(2):
                for h in range(2):
                    for j in range(CH):
                        r = h * W + j * FE
                        sp.dma_start(terms_r[r:r + FE, u, h, j, :], W1[2 * D:2 * D + FE, :]).then_inc(wef_in, 16)

            sp.wait_ge(base_ready, 1)
            for u in range(2):
                sp.wait_ge(B_out[u], 16 * SLOT_BLOCKS[u])

            def load_pair(k, u, t):
                last = is_last(k)
                sp.wait_ge(ohT_made, done(2 * k - 3))
                for h in range(2):
                    to = dst_bc[(1 - h) * W:(2 - h) * W, u, :]
                    if last and h:
                        sp.dma_start(to[:, 0:LAST_E], row(dst[(NG - 1) * GE:E]).to_broadcast([W, LAST_E])) \
                            .then_inc(dst_bc_in[u], 16)
                        sp.dma_start(to[:, LAST_E:GE], no_dst[:, :]).then_inc(dst_bc_in[u], 16)
                    else:
                        sp.dma_start(to, row(dst[ds((2 * k + h) * GE, GE)]).to_broadcast([W, GE])) \
                            .then_inc(dst_bc_in[u], 16)
                sp.wait_ge(pre_ps, done(2 * k - 3))
                for h in range(2):
                    at = sp.value_load(bases[0:1, ds(k, 1), 1 + h], min_val=0, max_val=NPAD - W)
                    sp.dma_start(terms_r[(1 - h) * W:(2 - h) * W, u, h, :, :],
                                 B_d[ds(at, W), :].unsqueeze(1).to_broadcast([W, CH, D])).then_inc(bwin_in[u], 16)
                sp.wait_ge(ef_turned, done(k - 2))
                to = ef_s[:, u, :].rearrange("p (h f) -> p h f", h=2)
                if last:
                    e0 = 2 * k * GE
                    sp.dma_start(to[:, 0, :], ef[e0:e0 + GE, :].rearrange("(p j) f -> p (j f)", j=CH)) \
                        .then_inc(ef_in[u], 16)
                    sp.dma_start(to[0:LAST_P, 1, :],
                                 ef[e0 + GE:E, :].rearrange("(p j) f -> p (j f)", j=CH)).then_inc(ef_in[u], 16)
                    sp.dma_start(to[LAST_P:P, 1, :],
                                 ef[0:GE - LAST_E, :].rearrange("(p j) f -> p (j f)", j=CH)) \
                        .then_inc(ef_in[u], 16)
                else:
                    sp.dma_start(to, ef[ds(2 * k * GE, 2 * GE), :].rearrange("(h p j) f -> p h (j f)", h=2, j=CH)) \
                        .then_inc(ef_in[u], 16)

            pairs(sp, (0, load_pair))

            blocks(sp, (0, load_block(x, xs, x2_in, xb_made)), (3, store_block(sp, As, x1_d, x1_out, x1_made)))
            landed(x1_out)

            blocks(sp, (0, load_block(x1_d, xs, x1_in, rb_made)), (1, load_block(x1_d, xr, xr_in, y_made)),
                   (3, store_block(sp, As, out, y_out, o_made)))
            landed(y_out)

        @block.gpsimd
        def _(pool):
            start_counters(pool, "pool")
            g = nc.gpsimd
            g.memset(ident[:, :], 0.0).then_inc(id_zero, 1)
            g.memset(ones[:, :], 1.0)
            g.memset(mhalf[:, :], -0.5)
            g.iota(iota_w[:, :], [[1, PW]], base=0, channel_multiplier=0, allow_small_or_imprecise_dtypes=True)
            g.iota(iota_p[:, :], [[0, 1]], base=0, channel_multiplier=1, allow_small_or_imprecise_dtypes=True)
            g.memset(lo[:, :], 0.0)
            g.memset(src_col[:, NG * CH:], 0)
            g.memset(dst_col[:, (NG - 1) * CH:], PAD_DST)
            pool.wait_ge(id_zero, 1)
            g.affine_select(out=ident[:, :], in_=ident[:, :], compare_op=ALU.not_equal, fill=1.0, base=0,
                            pattern=[[-1, P]], channel_multiplier=1).then_inc(consts, 1)
            g.memset(cdeg[:, :], 0.0)
            g.memset(no_dst[:, :], int(PAD_DST))
            g.memset(terms_r[:, :, :, :, :], 0.0).then_inc(wef_zero, 1)
            g.memset(S[:, :], 0.0)
            g.memset(T[:, :], 0.0).then_inc(zeroed, 1)

            for u in range(2):
                pool.wait_ge(A_out[u], 16 * SLOT_BLOCKS[u])

            def gather(table, staged, used, gathered, k, u):
                pool.wait_ge(staged, done(k))
                pool.nop(nofuse=True)
                for h in range(2):
                    pool.wait_ge(used, done(2 * k + (h - 4)) if used is pre_made else done(k - 2))
                    pool.nop(nofuse=True)
                    s = 2 * u + h
                    for j in range(CH):
                        g.indirect_dma_start(
                            out=gath[:, s, j * D:(j + 1) * D], out_offset=None, in_=table[0:N, :],
                            in_offset=bass.IndirectOffsetOnAxis(ap=idx[:, u, h * CH + j:h * CH + j + 1], axis=0),
                        ).then_inc(gathered[s], 16)

            pairs(pool, (0, lambda k, u, t: gather(A_d, staged0, pre_made, gathered0, k, u)))

            def inv_std(b, u, nt, n, stats, plus_eps, made):
                pool.wait_ge(stats, done(b))
                pool.nop(nofuse=True)
                g.tensor_scalar_add(ve[:, n, u, 0:nt], mv[:, n, u, 0:nt, 1], LN_EPS).then_inc(plus_eps, 1)
                pool.wait_ge(plus_eps, done(b))
                g.tensor_tensor(rstd[:, n, u, 0:nt], ve[:, n, u, 0:nt], mhalf[:, 0:nt], ALU.pow).then_inc(made, 1)

            blocks(pool, (0, lambda b, u, t, nt: inv_std(b, u, nt, 0, mv_made, ve_made, rstd_made)))

            for u in range(2):
                pool.wait_ge(x1_out[u], 16 * SLOT_BLOCKS[u])
            pairs(pool, (0, lambda k, u, t: gather(x1_d, staged1, agg_ps, gathered1, k, u)))

            def affine(b, u, t, nt):
                pool.wait_ge(rn_made, done(b))
                bc = [P, nt, D]
                g.tensor_tensor(nrm[:, u, 0:nt, :], nrm[:, u, 0:nt, :],
                                gamma_bc[:, :].unsqueeze(1).to_broadcast(bc), ALU.mult).then_inc(rg_made, 1)
                pool.wait_ge(rg_made, done(b))
                g.tensor_tensor(nrm[:, u, 0:nt, :], nrm[:, u, 0:nt, :],
                                beta_bc[:, :].unsqueeze(1).to_broadcast(bc), ALU.add).then_inc(rh_made, 1)

            blocks(pool, (0, lambda b, u, t, nt: inv_std(b, u, nt, 0, rmv_made, rve_made, rrstd_made)),
                   (1, affine), (2, lambda b, u, t, nt: inv_std(b, u, nt, 1, ymv_made, yve_made, yrstd_made)))

        @block.scalar
        def _(act):
            start_counters(act, "act")
            a = nc.scalar
            for to, of in ((w2[:, :], W2), (w3[:, :, :], W3.rearrange("(h k) n -> k h n", h=2)), (w4[:, :], W4),
                           (v1[:, :], V1), (v2[:, :], V2),
                           (b4_bc[:, :], row(b4).to_broadcast([P, D])), (c2_bc[:, :], row(c2).to_broadcast([P, D])),
                           (gamma_bc[:, :], row(gamma).to_broadcast([P, D])),
                           (beta_bc[:, :], row(beta).to_broadcast([P, D])),
                           (b2_col[:, :], col(b2)), (b3_col[:, :], col(b3)), (c1_col[:, :], col(c1)),
                           (one_eps[:, :], row(eps).to_broadcast([P, 1]))):
                act.dma_start(to, of).then_inc(w_in, 16)

            def keep_xT(b, u, t, nt):
                act.wait_ge(x_turned, done(b))
                act.wait_ge(ab_ps, done(b - 2))
                act.wait_ge(xT_kept, done(b - 2))
                a.copy(xTs[:, u, 0:nt * P], bank[u][:, 0:nt * P]).then_inc(xTs_made, 1)

            def keep_B(b, u, t, nt):
                act.wait_ge(A_made, done(b))
                if again(t):
                    act.wait_ge(B_out[u], 16 * t)
                for q in range(-(-nt // 2)):
                    n = min(2, nt - 2 * q)
                    last = a.copy(Bs[:, u, 2 * q:2 * q + n, :],
                                  bank[2 + 2 * u + q][:, :].rearrange("p (t d) -> p t d", t=2)[:, 0:n, D:])
                last.then_inc(B_made, 1)

            blocks(act, (0, keep_xT), (1, keep_B))

            def edge_features(k, u, t):
                act.wait_ge(ef_turned, done(k))
                act.wait_ge(pre_ps, done(2 * k - 3))
                for h in range(2):
                    r = slice(h * W, (h + 1) * W)
                    last = a.copy(terms_l[r, u, h, :, :], bank[4][r, 0:P].unsqueeze(1).to_broadcast([W, CH, P]))
                last.then_inc(efT_made, 1)

            def messages(k, u, t):
                for h in range(2):
                    g = 2 * k + h
                    act.wait_ge(pre_made, done(g))
                    act.wait_ge(sums_ps, done(k - 2))
                    a.activation(msg[:, 2 * u + h, :], pre[:, h, :], ACT.Silu).then_inc(msg_made, 1)

            pairs(act, (0, edge_features), (1, messages))

            act.wait_ge(w_in, 16 * 13)

            def hidden0(b, u, t, nt):
                act.wait_ge(upd_ps, done(b))
                act.wait_ge(hnew_ps, done(b - 2))
                a.activation(hid[:, u, 0:nt * P], bank[u][:, 0:nt * P], ACT.Silu,
                             bias=b3_col[:, :]).then_inc(hid_made, 1)

            def start_T(b, u, t, nt):
                act.wait_ge(x1_turned, done(b))
                a.activation(T[:, cols(b, nt)], bank[4 + u][:, 0:nt * P], ACT.Copy,
                             scale=one_eps[:, :]).then_inc(T_init, 1)

            act.wait_ge(dst_ready, 3)
            blocks(act, (0, hidden0), (3, start_T))

            def hidden1(b, u, t, nt):
                act.wait_ge(z_ps, done(b))
                act.wait_ge(r_ps, done(b - 2))
                a.activation(hid[:, u, 0:nt * P], bank[u][:, 0:nt * P], ACT.Relu,
                             bias=c1_col[:, :]).then_inc(z_made, 1)

            blocks(act, (0, hidden1))

        @block.tensor
        def _(pe):
            start_counters(pe, "pe")
            mm = nc.tensor.matmul

            def turn_rows(prep, turned):
                pe.wait_ge(prep, 1)
                for q, n in ((0, P), (1, GT)):
                    for j in range(CH):
                        last = nc.tensor.transpose(
                            bank[6 + q][:, j * P:j * P + n],
                            rows_f[0:n, q, :].rearrange("g (p j) -> g j p", j=CH)[:, j, :], ident[0:n, 0:n])
                last.then_inc(turned, 1)

            pe.wait_ge(consts, 1)
            turn_rows(src_prep, src_turned)
            pe.wait_ge(wab_in, 16 * 3)

            def turn_x(b, u, t, nt):
                pe.wait_ge(x_in[u], 16 * (t + 1))
                pe.wait_ge(xTs_made, done(b - 2))
                for j in range(nt):
                    last = nc.tensor.transpose(bank[u][:, j * P:(j + 1) * P], xs[:, u, j, :], ident[:, :])
                last.then_inc(x_turned, 1)

            def terms(b, u, t, nt):
                pe.wait_ge(xTs_made, done(b))
                pe.wait_ge(B_made, done(b - 2))
                for j in range(nt):
                    last = mm(bank[2 + 2 * u + j // 2][:, (j % 2) * 2 * D:(j % 2 + 1) * 2 * D],
                              xTs[:, u, j * P:(j + 1) * P], wab[:, :], start=True, stop=True)
                last.then_inc(ab_ps, 1)

            blocks(pe, (0, turn_x), (1, terms))

            pe.wait_ge(src_ready, 1)
            turn_rows(dst_prep, dst_turned)
            pe.wait_ge(dst_ready, 1)
            mm(bank[0][:, 0:2 * P], ones[:, :], base_diag[:, :, :].rearrange("p q g -> p (q g)"),
               start=True, stop=True).then_inc(base_turned, 1)
            pe.wait_ge(w_in, 16 * 13)
            nc.tensor.transpose(bank[1][:, 0:D], w2[:, :], ident[:, :]).then_inc(w2_turned, 1)
            pe.wait_ge(w2_ready, 1)
            mm(bank[1][:, D:2 * D], w2t[:, :], w3[:, 1, :], start=True, stop=True)
            mm(bank[1][0:1, 2 * D:3 * D], b2_col[:, :], w3[:, 1, :], start=True, stop=True).then_inc(w23_ps, 1)
            pe.wait_ge(w23_ready, 1)
            pe.wait_ge(B_made, done(NB))
            pe.wait_ge(wef_in, 16 * 4 * CH)

            def turn_ef(k, u, t):
                pe.wait_ge(ef_in[u], 16 * (t + 1) if not is_last(k) else 16 * (t + 3))
                pe.wait_ge(efT_made, done(k - 1))
                nc.tensor.transpose(bank[4][:, 0:P], ef_s[:, u, :], ident[:, :]).then_inc(ef_turned, 1)

            def pre_sums(k, u, t):
                pe.wait_ge(efT_made, done(k))
                pe.wait_ge(bwin_in[u], 32 * (t + 1))
                pe.wait_ge(ohT_made, done(2 * k + 1))
                for h in range(2):
                    pe.wait_ge(pre_made, done(2 * k + h - 2))
                    for j in range(CH):
                        last = mm(bank[h][:, j * D:(j + 1) * D], terms_l[:, u, h, j, :], terms_r[:, u, h, j, :],
                                  start=True, stop=True)
                    last.then_inc(pre_ps, 1)

            def message_sums(k, u, t):
                pe.wait_ge(sums_added, done(k - 2))
                for c in range(2 * CH):
                    if c % CH == 0:
                        pe.wait_ge(msg_made, done(2 * k + c // CH))
                    mm(bank[2 + u][:, 0:PW], msg[:, 2 * u + c // CH, c % CH * D:(c % CH + 1) * D], oh[:, u, c, :],
                       start=c == 0, stop=c == 2 * CH - 1)
                mm(bank[2 + u][0:1, PW:2 * PW], deg_col[:, u:u + 1], ident[:, :],
                   start=True, stop=True).then_inc(sums_ps, 1)

            pairs(pe, (0, turn_ef), (1, pre_sums), (2, message_sums))

            pe.wait_ge(sums_added, done(NPAIR - 1))
            pe.wait_ge(xT_kept, done(NB))

            def hidden0(b, u, t, nt):
                n = nt * P
                pe.wait_ge(hid_made, done(b - 2))
                mm(bank[u][:, 0:n], w3[:, 0, :], xT[:, cols(b, nt)], start=True, stop=False)
                mm(bank[u][:, 0:n], w23[:, :], S[:, cols(b, nt)], start=False, stop=False)
                mm(bank[u][:, 0:n], cdeg[:, :], T[:, cols(b, nt)], start=False, stop=True).then_inc(upd_ps, 1)

            def out0(b, u, t, nt):
                pe.wait_ge(hid_made, done(b))
                pe.wait_ge(v_made, done(b - 2))
                for j in range(nt):
                    last = mm(bank[2 + u][:, j * D:(j + 1) * D], hid[:, u, j * P:(j + 1) * P], w4[:, :],
                              start=True, stop=True)
                last.then_inc(hnew_ps, 1)

            def turn_x1(b, u, t, nt):
                pe.wait_ge(x1_made, done(b))
                pe.wait_ge(T_init, done(b - 2))
                for j in range(nt):
                    last = nc.tensor.transpose(bank[4 + u][:, j * P:(j + 1) * P], As[:, u, j, :], ident[:, :])
                last.then_inc(x1_turned, 1)

            blocks(pe, (3, turn_x1), (1, out0), (0, hidden0))

            def neighbour_sums(k, u, t):
                pe.wait_ge(oh1_made, done(k))
                pe.wait_ge(agg_added, done(k - 2))
                for c in range(2 * CH):
                    s = 2 * u + c // CH
                    if c % CH == 0:
                        pe.wait_ge(gathered1[s], 16 * CH * (t + 1))
                    last = mm(bank[2 + u][:, 0:PW], gath[:, s, c % CH * D:(c % CH + 1) * D], oh[:, u, c, :],
                              start=c == 0, stop=c == 2 * CH - 1)
                last.then_inc(agg_ps, 1)

            pe.wait_ge(v_made, done(NB))
            pairs(pe, (0, neighbour_sums))

            pe.wait_ge(agg_added, done(NPAIR - 1))

            def hidden1(b, u, t, nt):
                n = nt * P
                pe.wait_ge(z_made, done(b - 2))
                mm(bank[u][:, 0:n], v1[:, :], T[:, cols(b, nt)], start=True, stop=True).then_inc(z_ps, 1)

            def out1(b, u, t, nt):
                pe.wait_ge(z_made, done(b))
                pe.wait_ge(r_made, done(b - 2))
                for j in range(nt):
                    last = mm(bank[4 + u][:, j * D:(j + 1) * D], hid[:, u, j * P:(j + 1) * P], v2[:, :],
                              start=True, stop=True)
                last.then_inc(r_ps, 1)

            pe.wait_ge(T_init, done(NB))
            blocks(pe, (1, out1), (0, hidden1))

        @block.vector
        def _(dve):
            start_counters(dve, "dve")
            ve_ = nc.vector

            def cols_of(q, col, made):
                g0, n = (0, P) if q == 0 else (P, GT - 1)
                ps = bank[6 + q][:, :].rearrange("p (j g) -> p g j", j=CH)
                ve_.tensor_copy(col[:, g0 * CH:(g0 + n) * CH].rearrange("p (g j) -> p g j", j=CH), ps[:, 0:n, :])
                if q:
                    last_p = LAST_P if col is dst_col else P
                    return ve_.tensor_copy(col[0:last_p, (NG - 1) * CH:NG * CH], ps[0:last_p, n, :])

            def to_float(rows, landed, made):
                dve.wait_ge(landed, 16 * 4)
                ve_.tensor_copy(rows_f[:, 0, :], rows[:, 0, :])
                ve_.tensor_copy(rows_f[0:GT, 1, :], rows[0:GT, 1, :]).then_inc(made, 1)

            to_float(src_rows, src_in, src_prep)
            dve.wait_ge(consts, 1)
            dve.wait_ge(src_turned, 1)
            cols_of(0, src_col, None)
            cols_of(1, src_col, None).then_inc(src_ready, 1)

            dve.wait_ge(wab_in, 16 * 3)

            def keep_xT(b, u, t, nt):
                dve.wait_ge(xTs_made, done(b))
                ve_.tensor_copy(xT[:, cols(b, nt)], xTs[:, u, 0:nt * P]).then_inc(xT_kept, 1)

            def keep_A(b, u, t, nt):
                dve.wait_ge(ab_ps, done(b))
                if again(t):
                    dve.wait_ge(A_out[u], 16 * t)
                for q in range(-(-nt // 2)):
                    n = min(2, nt - 2 * q)
                    last = ve_.tensor_tensor(
                        As[:, u, 2 * q:2 * q + n, :],
                        bank[2 + 2 * u + q][:, :].rearrange("p (t d) -> p t d", t=2)[:, 0:n, 0:D],
                        b1_bc[:, :].unsqueeze(1).to_broadcast([P, n, D]), ALU.add)
                last.then_inc(A_made, 1)

            blocks(dve, (0, keep_xT), (1, keep_A))

            def stage(k, u, staged):
                ve_.tensor_copy(idx[:, u, :], src_col[:, ds(k * (2 * CH), 2 * CH)]).then_inc(staged, 1)

            dve.wait_ge(src_ready, 1)
            for u in range(2):
                stage(u, u, staged0)

            dve.wait_ge(src_turned, 1)
            to_float(dst_rows, dst_in, dst_prep)
            dve.wait_ge(dst_prep, 1)
            dve.wait_ge(consts, 1)
            ve_.tensor_reduce(lo[:, 0:1], rows_f[:, 0, :], AX_X, ALU.min)
            ve_.tensor_reduce(lo[0:GT, 1:2], rows_f[0:GT, 1, :], AX_X, ALU.min).then_inc(rel_ready, 1)
            dve.wait_ge(rel_ready, 1)
            for q in range(2):
                last = ve_.tensor_scalar(base_diag[:, q, :], ident[:, :], lo[:, q:q + 1], float(NPAD - W),
                                         ALU.mult, ALU.min)
            last.then_inc(dst_ready, 1)
            dve.wait_ge(dst_turned, 1)
            cols_of(0, dst_col, None)
            cols_of(1, dst_col, None).then_inc(dst_ready, 1)
            dve.wait_ge(w_in, 16 * 13)
            ve_.tensor_scalar_add(one_eps[:, :], one_eps[:, :], 1.0).then_inc(dst_ready, 1)
            dve.wait_ge(base_turned, 1)
            ve_.tensor_copy(base_bc[:, :], bank[0][:, 0:2 * P]).then_inc(rel_ready, 1)
            dve.wait_ge(rel_ready, 2)
            by_pair = base_bc[:, 0:NG].rearrange("p (k h) -> p k h", h=2)
            ve_.tensor_tensor(pair_bc[:, :], by_pair[:, :, 0], by_pair[:, :, 1], ALU.min).then_inc(rel_ready, 1)
            dve.wait_ge(rel_ready, 3)
            ve_.tensor_scalar(pair_bc[:, :], pair_bc[:, :], float(NPAD - PW), None, ALU.min).then_inc(rel_ready, 1)
            for h in range(2):
                ve_.tensor_copy(bases[:, :, 1 + h], by_pair[0:1, :, h])
            dve.wait_ge(rel_ready, 4)
            ve_.tensor_copy(bases[:, :, 0], pair_bc[0:1, :]).then_inc(base_ready, 1)
            dve.wait_ge(dst_ready, 3)
            ve_.tensor_tensor(dst_rel[:, :].rearrange("p (k c) -> p k c", c=2 * CH),
                              dst_col[:, :].rearrange("p (k c) -> p k c", c=2 * CH),
                              pair_bc[:, :].unsqueeze(2).to_broadcast([P, NPAIR, 2 * CH]), ALU.subtract)
            for h in range(2):
                r = slice((1 - h) * W, (2 - h) * W)
                last = ve_.tensor_scalar(node_col[r, :], by_pair[r, :, h], iota_p[r, :], float((h - 1) * W),
                                         ALU.add, ALU.add)
            last.then_inc(rel_ready, 1)
            dve.wait_ge(w2_turned, 1)
            ve_.tensor_copy(w2t[:, :], bank[1][:, 0:D]).then_inc(w2_ready, 1)
            dve.wait_ge(w23_ps, 1)
            ve_.tensor_copy(w23[:, :], bank[1][:, D:2 * D])
            dve.wait_ge(wef_zero, 1)
            ve_.tensor_copy(cdeg[0:1, :], bank[1][0:1, 2 * D:3 * D]).then_inc(w23_ready, 1)
            dve.wait_ge(rel_ready, 5)
            dve.wait_ge(zeroed, 1)

            def one_hots(k, u, read, made):
                dve.wait_ge(read, done(k - 2))
                shape = [P, 2 * CH, PW]
                ve_.tensor_tensor(oh[:, u, :, :], iota_w[:, :].unsqueeze(1).to_broadcast(shape),
                                  dst_rel[:, ds(k * (2 * CH), 2 * CH)].unsqueeze(2).to_broadcast(shape),
                                  ALU.is_equal).then_inc(made, 1)

            def windows(k, u, t):
                dve.wait_ge(dst_bc_in[u], 32 * (t + 1) + (16 if is_last(k) else 0))
                dve.wait_ge(pre_ps, done(2 * k - 3))
                dve.wait_ge(sums_ps, done(k - 2))
                for h in range(2):
                    r = slice((1 - h) * W, (2 - h) * W)
                    ve_.tensor_scalar(terms_l[r, u, h, :, :],
                                      dst_bc[r, u, :].rearrange("n (p j) -> n j p", j=CH), node_col[r, ds(k, 1)],
                                      None, ALU.is_equal, ALU.add, accum_out=deg_col[r, u:u + 1]).then_inc(ohT_made, 1)

            def source_terms(k, u, t):
                for h in range(2):
                    g = 2 * k + h
                    s = 2 * u + h
                    dve.wait_ge(gathered0[s], 16 * CH * (t + 1))
                    dve.wait_ge(pre_ps, done(g))
                    dve.wait_ge(msg_made, done(g - 2))
                    ve_.tensor_tensor(pre[:, h, :], bank[h][:, :], gath[:, s, :], ALU.add).then_inc(pre_made, 1)
                stage(k + 2, u, staged0)

            def add_sums(k, u, t):
                at, at0, at1 = [dve.value_load(bases[0:1, ds(k, 1), i], min_val=0, max_val=NPAD - (W if i else PW))
                                for i in range(3)]
                dve.wait_ge(sums_ps, done(k))
                dve.wait_ge(sums_added, done(k - 1))
                ve_.tensor_tensor(S[:, ds(at, PW)], S[:, ds(at, PW)], bank[2 + u][:, 0:PW], ALU.add)
                ve_.tensor_tensor(T[0:1, ds(at0, W)], T[0:1, ds(at0, W)],
                                  bank[2 + u][0:1, PW + W:2 * PW], ALU.add).then_inc(deg_added, 1)
                dve.wait_ge(deg_added, done(k))
                ve_.tensor_tensor(T[0:1, ds(at1, W)], T[0:1, ds(at1, W)],
                                  bank[2 + u][0:1, PW:PW + W], ALU.add).then_inc(sums_added, 1)

            pairs(dve, (1, source_terms), (0, windows), (0, lambda k, u, t: one_hots(k, u, sums_ps, oh_made)),
                  (2, add_sums))

            dve.wait_ge(w_in, 16 * 13)

            def stats(b, nt, u, n, of, read, raw, made):
                dve.wait_ge(read, done(b))
                for j in range(nt):
                    last = ve_.bn_stats(st[:, n, u, j, :], of[:, u, j, :])
                last.then_inc(raw, 1)
                dve.wait_ge(raw, done(b))
                dve.nop(nofuse=True)
                for j in range(nt):
                    last = ve_.bn_aggr(mv[:, n, u, j, :], st[:, n, u, j, :])
                last.then_inc(made, 1)

            def normalise(b, nt, u, n, to, of, inv, made):
                dve.wait_ge(inv, done(b))
                for j in range(nt):
                    last = ve_.tensor_scalar(to[:, u, j, :], of[:, u, j, :], mv[:, n, u, j, 0:1],
                                             rstd[:, n, u, j:j + 1], ALU.subtract, ALU.mult)
                last.then_inc(made, 1)

            def skip0(b, u, t, nt):
                dve.wait_ge(x2_in[u], 16 * (t + 1))
                bc = b4_bc[:, :].unsqueeze(1).to_broadcast([P, nt, D])
                ve_.scalar_tensor_tensor(out=v[:, u, 0:nt, :], in0=xs[:, u, 0:nt, :], scalar=2.0, in1=bc,
                                         op0=ALU.mult, op1=ALU.add).then_inc(xb_made, 1)

            def rows0(b, u, t, nt):
                dve.wait_ge(xb_made, done(b))
                dve.wait_ge(hnew_ps, done(b))
                ve_.tensor_tensor(v[:, u, 0:nt, :], bank[2 + u][:, 0:nt * D].rearrange("p (t d) -> p t d", d=D),
                                  v[:, u, 0:nt, :], ALU.add).then_inc(v_made, 1)
                stats(b, nt, u, 0, v, v_made, st_made, mv_made)

            def norm0(b, u, t, nt):
                if again(t):
                    dve.wait_ge(x1_out[u], 16 * t)
                dve.wait_ge(x1_turned, done(b - 2))
                normalise(b, nt, u, 0, As, v, rstd_made, x1_made)

            for u in range(2):
                dve.wait_ge(A_out[u], 16 * SLOT_BLOCKS[u])
            blocks(dve, (2, norm0), (1, rows0), (0, skip0))

            for u in range(2):
                stage(u, u, staged1)
            dve.wait_ge(T_init, done(NB))

            def add_neighbours(k, u, t):
                at = dve.value_load(bases[0:1, ds(k, 1), 0], min_val=0, max_val=NPAD - PW)
                dve.wait_ge(agg_ps, done(k))
                dve.wait_ge(agg_added, done(k - 1))
                ve_.tensor_tensor(T[:, ds(at, PW)], T[:, ds(at, PW)], bank[2 + u][:, 0:PW],
                                  ALU.add).then_inc(agg_added, 1)
                stage(k + 2, u, staged1)

            pairs(dve, (0, lambda k, u, t: one_hots(k, u, agg_ps, oh1_made)), (0, add_neighbours))

            def skip1(b, u, t, nt):
                dve.wait_ge(x1_in[u], 16 * (t + 1))
                bc = c2_bc[:, :].unsqueeze(1).to_broadcast([P, nt, D])
                ve_.tensor_tensor(v[:, u, 0:nt, :], xs[:, u, 0:nt, :], bc, ALU.add).then_inc(rb_made, 1)

            def rows1(b, u, t, nt):
                dve.wait_ge(rb_made, done(b))
                dve.wait_ge(r_ps, done(b))
                ve_.tensor_tensor(v[:, u, 0:nt, :], bank[4 + u][:, 0:nt * D].rearrange("p (t d) -> p t d", d=D),
                                  v[:, u, 0:nt, :], ALU.add).then_inc(r_made, 1)
                stats(b, nt, u, 0, v, r_made, rst_made, rmv_made)

            def norm1(b, u, t, nt):
                normalise(b, nt, u, 0, nrm, v, rrstd_made, rn_made)

            def rows2(b, u, t, nt):
                dve.wait_ge(xr_in[u], 16 * (t + 1))
                dve.wait_ge(rh_made, done(b))
                ve_.scalar_tensor_tensor(out=y[:, u, 0:nt, :], in0=nrm[:, u, 0:nt, :], scalar=0.0,
                                         in1=xr[:, u, 0:nt, :], op0=ALU.max, op1=ALU.add).then_inc(y_made, 1)
                stats(b, nt, u, 1, y, y_made, yst_made, ymv_made)

            def norm2(b, u, t, nt):
                if again(t):
                    dve.wait_ge(y_out[u], 16 * t)
                normalise(b, nt, u, 1, As, y, yrstd_made, o_made)

            blocks(dve, (3, norm2), (2, rows2), (1, norm1), (0, skip1), (0, rows1))


_INS = ['x', 'src', 'dst', 'edge_attr_16', 'L0_gnn_W1', 'L0_gnn_b1', 'L0_gnn_W2', 'L0_gnn_b2', 'L0_gnn_W3',
        'L0_gnn_b3', 'L0_gnn_W4', 'L0_gnn_b4', 'L1_gnn_eps', 'L1_gnn_W1', 'L1_gnn_b1', 'L1_gnn_W2', 'L1_gnn_b2',
        'L1_gnn_gamma', 'L1_gnn_beta']


def kernel(**inputs):
    import numpy as np
    import concourse.bacc as bacc
    from concourse.bass_utils import run_bass_kernel_spmd

    nc = bacc.Bacc("TRN2", target_bir_lowering=False, num_devices=1)
    arrays, args = {}, []
    for name in _INS:
        a = np.ascontiguousarray(inputs[name])
        if a.ndim == 0:
            a = a.reshape(1)
        arrays[f"in_{name}"] = a
        args.append(nc.dram_tensor(f"in_{name}", a.shape, mybir.dt.from_np(a.dtype), kind="ExternalInput").ap())
    out = nc.dram_tensor("out", tuple(inputs["x"].shape), F32, kind="ExternalOutput").ap()
    build(nc, *args, out)
    r = run_bass_kernel_spmd(nc, [arrays], core_ids=[0])
    return r.results[0]["out"]
```

```python
from contextlib import ExitStack

import concourse.bass as bass
from concourse import mybir

ACT = mybir.ActivationFunctionType
ALU = mybir.AluOpType
AX_X = mybir.AxisListType.X
F32 = mybir.dt.float32
I32 = mybir.dt.int32
ds = bass.ds

P = 128
D = 128
FE = 16
CH = 4
GE = CH * P
W = 64
PW = 2 * W
BT = 4
BN = BT * P
START = 4
PAD_DST = -1000.0
LN_EPS = 1e-5


def done(n):
    return n + 1 + START


def landed(n):
    return 16 * (n + 1) + START


def build(nc, x, src, dst, ef, W1, b1, W2, b2, W3, b3, W4, b4, eps, V1, c1, V2, c2, gamma, beta, out):
    N, E = x.shape[0], src.shape[0]
    NG = -(-E // GE)
    NPAIR = NG // 2
    assert NG % 4 == 0 and N % P and NG > P
    NT = -(-N // P)
    NPAD = NT * P
    NB = NT // BT
    TAIL = NT - NB * BT
    assert TAIL == 1 and NB % 2 == 0
    LAST_ROWS = N - (NT - 1) * P
    assert NPAIR == 2 * NT
    LAST_E = E - (NG - 1) * GE
    LAST_P = LAST_E // CH
    assert LAST_E % CH == 0
    GT = NG - P

    A_d = nc.dram_tensor("src_term", (NPAD, D), F32).ap()
    B_d = nc.dram_tensor("dst_term", (NPAD, D), F32).ap()
    x1_d = nc.dram_tensor("layer1_input", (NPAD, D), F32).ap()

    with ExitStack() as ctx:
        def sb(name, shape, dt=F32):
            return ctx.enter_context(nc.sbuf_tensor(name, shape, dt))

        def sem(name):
            return ctx.enter_context(nc.semaphore(name))

        counters = {}

        def counter(name, engine):
            counters.setdefault(engine, []).append(sem(name))
            return counters[engine][-1]

        ident = sb("ident", [P, P])
        ones = sb("ones", [P, P])
        iota_w = sb("iota_w", [P, PW])
        iota_p = sb("iota_p", [P, 1])
        tile_end = sb("tile_end", [P, NPAIR])
        mhalf = sb("mhalf", [P, 2])
        var_eps = sb("var_eps", [P, 2])
        eps_col = sb("eps_col", [P, 1])
        wab = sb("wab", [P, 2 * D])
        wef = sb("wef", [P, D])
        own_rows = sb("own_rows", [P, P // FE])
        w2 = sb("w2", [P, D])
        w2t = sb("w2t", [P, D])
        w3 = sb("w3", [P, 2, D])
        w23 = sb("w23", [P, D])
        cdeg = sb("cdeg", [P, D])
        w4 = sb("w4", [P, D])
        v1 = sb("v1", [P, D])
        v2 = sb("v2", [P, D])
        b1_bc = sb("b1_bc", [P, D])
        b4_bc = sb("b4_bc", [P, D])
        c2_bc = sb("c2_bc", [P, D])
        gamma_bc = sb("gamma_bc", [P, D])
        beta_bc = sb("beta_bc", [P, D])
        b2_col = sb("b2_col", [P, 1])
        b3_col = sb("b3_col", [P, 1])
        c1_col = sb("c1_col", [P, 1])
        one_eps = sb("one_eps", [P, 1])
        src_rows = sb("src_rows", [P, 2, GE], I32)
        dst_rows = sb("dst_rows", [P, 2, GE], I32)
        src_rows_f = sb("src_rows_f", [P, 2, GE])
        dst_rows_f = sb("dst_rows_f", [P, 2, GE])
        src_col = sb("src_col", [P, (NG + 4) * CH], I32)
        dst_col = sb("dst_col", [P, NG * CH])
        dst_rel = sb("dst_rel", [P, NG * CH])
        past = sb("past", [P, NG * CH])
        lo = sb("lo", [P, 2])
        base_diag = sb("base_diag", [P, 2, P])
        base_bc = sb("base_bc", [P, 2 * P])
        pair_bc = sb("pair_bc", [P, NPAIR])
        early = sb("early", [P, NPAIR])
        misfits = sb("misfits", [P, 2])
        misfit_count = sb("misfit_count", [1, 2], I32)
        no_dst = sb("no_dst", [W, GE - LAST_E], I32)
        bases = sb("bases", [1, NPAIR, 4], I32)
        node_col = sb("node_col", [P, NPAIR])
        xT = sb("xT", [P, NPAD])
        S = sb("S", [P, NPAD])
        T = sb("T", [P, NPAD])
        xs = sb("xs", [P, 2, BT, D])
        xTs = sb("xTs", [P, 2, BN])
        As = sb("As", [P, 2, BT, D])
        idx = sb("idx", [P, 2, 2 * CH], I32)
        xw = sb("xw", [P, 2 * W])
        gath = sb("gath", [P, 4, CH * D])
        dst_bc = sb("dst_bc", [P, 2, GE], I32)
        terms_l = sb("terms_l", [P, 2, 2, CH, P])
        terms_r = sb("terms_r", [P, 2, 2, CH, D])
        deg_col = sb("deg_col", [P, 2])
        ef_s = sb("ef_s", [P, 2, 2 * CH * FE])
        oh = sb("oh", [P, 2, 2 * CH, PW])
        pre = sb("pre", [P, 2, CH * D])
        msg = sb("msg", [P, 4, CH * D])
        any_b = sb("any_b", [P, D])
        any_rel = sb("any_rel", [P, CH])
        xt = sb("xt", [P, 2, D])
        hid = sb("hid", [P, 2 * P])
        v = sb("v", [P, 2, D])
        nrm = sb("nrm", [P, 2, 2, D])
        y = sb("y", [P, 2, D])
        ot = sb("ot", [P, 2, D])
        st = sb("st", [P, 2, 2, 6])
        mv = sb("mv", [P, 2, 2, 2])
        std = sb("std", [P, 2, 2])
        rstd = sb("rstd", [P, 2, 2])

        bank = [ctx.enter_context(nc.psum_tensor(f"bank{i}", [P, 512], F32)) for i in range(8)]

        wab_in = sem("wab_in")
        src_in = sem("src_in")
        dst_in = sem("dst_in")
        wef_in = sem("wef_in")
        w_in = sem("w_in")
        x_in = [sem(f"x_in{u}") for u in range(2)]
        A_out = [sem(f"A_out{u}") for u in range(2)]
        gathered0 = [sem(f"gathered0_{s}") for s in range(4)]
        gathered1 = [sem(f"gathered1_{s}") for s in range(4)]
        dst_bc_in = [sem(f"dst_bc_in{u}") for u in range(2)]
        ef_in = [sem(f"ef_in{u}") for u in range(2)]
        id_zero = sem("id_zero")
        consts = sem("consts")
        zeroed = sem("zeroed")
        own_rows_made = sem("own_rows_made")
        wef_ready = sem("wef_ready")
        src_prep = sem("src_prep")
        src_turned = sem("src_turned")
        src_ready = sem("src_ready")
        dst_prep = sem("dst_prep")
        dst_turned = sem("dst_turned")
        dst_ready = sem("dst_ready")
        lo_made = sem("lo_made")
        diag_made = sem("diag_made")
        base_turned = sem("base_turned")
        base_steps = sem("base_steps")
        base_ready = sem("base_ready")
        rel_ready = sem("rel_ready")
        past_made = sem("past_made")
        early_made = sem("early_made")
        misfits_made = sem("misfits_made")
        misfits_summed = sem("misfits_summed")
        order_known = sem("order_known")
        one_eps_made = sem("one_eps_made")
        w2_turned = sem("w2_turned")
        w2_ready = sem("w2_ready")
        w23_ps = sem("w23_ps")
        w23_ready = sem("w23_ready")
        x_turned = counter("x_turned", "pe")
        xTs_made = counter("xTs_made", "act")
        xT_kept = counter("xT_kept", "dve")
        ab_ps = counter("ab_ps", "pe")
        A_made = counter("A_made", "dve")
        staged0 = counter("staged0", "dve")
        ohT_made = counter("ohT_made", "dve")
        oh_made = counter("oh_made", "dve")
        xw_made = counter("xw_made", "act")
        ef_turned = counter("ef_turned", "pe")
        efT_made = counter("efT_made", "act")
        pre_ps = counter("pre_ps", "pe")
        pre_made = counter("pre_made", "dve")
        msg_made = counter("msg_made", "act")
        sums_ps = counter("sums_ps", "pe")
        deg_added = counter("deg_added", "dve")
        sums_added = counter("sums_added", "dve")
        staged1 = counter("staged1", "dve")
        oh1_made = counter("oh1_made", "dve")
        agg_ps = counter("agg_ps", "pe")
        agg_added = counter("agg_added", "dve")
        any_xw_made = counter("any_xw_made", "act")
        any_b_ps = counter("any_b_ps", "pe")
        any_b_made = counter("any_b_made", "act")
        any_b_out = counter("any_b_out", "act")
        any_copied = counter("any_copied", "dve")
        any_staged = counter("any_staged", "dve")
        any_ef_in = counter("any_ef_in", "sp")
        any_src_in = sem("any_src_in")
        any_dst_in = sem("any_dst_in")
        any_ef_turned = counter("any_ef_turned", "pe")
        any_efT_made = counter("any_efT_made", "act")
        any_pre_ps = counter("any_pre_ps", "pe")
        any_ab_made = counter("any_ab_made", "dve")
        any_pre_made = counter("any_pre_made", "dve")
        any_msg_made = counter("any_msg_made", "act")
        any_oh_made = counter("any_oh_made", "dve")
        any_moved = counter("any_moved", "dve")
        any_ps = counter("any_ps", "pe")
        any_added = counter("any_added", "dve")
        any1_copied = counter("any1_copied", "dve")
        any1_staged = counter("any1_staged", "dve")
        any1_x1_in = sem("any1_x1_in")
        any1_oh_made = counter("any1_oh_made", "dve")
        any1_moved = counter("any1_moved", "dve")
        any1_ps = counter("any1_ps", "pe")
        any1_added = counter("any1_added", "dve")
        xt_in = counter("xt_in", "sp")
        upd_ps = counter("upd_ps", "pe")
        hid_made = counter("hid_made", "act")
        hnew_ps = counter("hnew_ps", "pe")
        xb_made = counter("xb_made", "dve")
        v_made = counter("v_made", "dve")
        st_made = counter("st_made", "dve")
        mv_made = counter("mv_made", "dve")
        std_made = counter("std_made", "act")
        rstd_made = counter("rstd_made", "dve")
        var_eps_made = counter("var_eps_made", "pool")
        pool_rstd_made = counter("pool_rstd_made", "pool")
        x1_made = counter("x1_made", "dve")
        x1_out = counter("x1_out", "act")
        x1_turned = counter("x1_turned", "pe")
        T_init = counter("T_init", "act")
        x1_in = counter("x1_in", "sp")
        z_ps = counter("z_ps", "pe")
        z_made = counter("z_made", "act")
        r_ps = counter("r_ps", "pe")
        rb_made = counter("rb_made", "dve")
        r_made = counter("r_made", "dve")
        rst_made = counter("rst_made", "dve")
        rmv_made = counter("rmv_made", "dve")
        rstd1_made = counter("rstd1_made", "act")
        rinv_made = counter("rinv_made", "dve")
        rg_made = counter("rg_made", "dve")
        rh_made = counter("rh_made", "dve")
        y_made = counter("y_made", "dve")
        yst_made = counter("yst_made", "dve")
        ymv_made = counter("ymv_made", "dve")
        ystd_made = counter("ystd_made", "act")
        yinv_made = counter("yinv_made", "dve")
        o_made = counter("o_made", "dve")
        o_out = counter("o_out", "act")

        def start_counters(eng, name):
            for s in counters.get(name, []):
                eng.sem_inc(s, START)

        def of_unit(lag, body):
            return lag, body, True

        def skewed(eng, items, stages, loop_to):
            reach = max(stage[0] for stage in stages)

            def step(s, parity, half):
                for lag, body, *unit in stages:
                    slot = (parity - lag) % 2
                    if unit and not slot:
                        if not isinstance(s, int):
                            body(half + (parity - lag) // 2)
                        elif 0 <= (s - lag) // 2 < UNITS:
                            body((s - lag) // 2)
                    elif not unit:
                        if not isinstance(s, int):
                            body(2 * half + (parity - lag), slot, half + (parity - lag - slot) // 2)
                        elif 0 <= s - lag < items:
                            body(s - lag, slot, (s - lag) // 2)

            first = 2 + reach + reach % 2
            for s in range(first):
                step(s, s % 2, None)
            with eng.Fori(first // 2, loop_to // 2) as half:
                for parity in range(2):
                    step(None, parity, half)
            for s in range(loop_to, items + reach):
                step(s, s % 2, None)

        def blocks(eng, *stages):
            def sized(body):
                return lambda b, u, t: body(b, u, t, TAIL if isinstance(b, int) and b == NB else BT)
            skewed(eng, NB + 1, [(lag, sized(body)) for lag, body in stages], NB)

        def only_at(parts):
            return lambda i, *_: parts[i]() if isinstance(i, int) and i in parts else None

        def pairs(eng, *stages):
            skewed(eng, NPAIR, stages, NPAIR - 2)

        def is_last(k):
            return isinstance(k, int) and k == NPAIR - 1

        def again(t):
            return not (isinstance(t, int) and t == 0)

        def tiles(j):
            return 2 if isinstance(j, int) and j == UNITS - 1 else 1

        def moved(j):
            return landed(j + (tiles(j) - 1))

        def last_pair(j):
            return min(2 * j + 3, NPAIR - 1) if isinstance(j, int) else 2 * j + 3

        def rsqrt_on_pool(j):
            return isinstance(j, int) and j >= FIRST_ON_POOL

        def either_order(eng, ordered, any_order):
            eng.wait_ge(order_known, 1)
            n = [eng.value_load(misfit_count[0:1, i:i + 1], min_val=0, max_val=P * NPAIR + E) for i in range(2)]
            with eng.If(n[0] + n[1] > 0):
                any_order()
            with eng.Else():
                ordered()

        def all_groups(eng, group, tile=None):
            with eng.Fori(0, NG) as i:
                group(i)
                if tile:
                    with eng.Fori(0, NT) as w:
                        tile(w, i * NT + w)
                    eng.nop(nofuse=True)

        def all_units(eng, *bodies):
            with eng.Fori(0, UNITS - 1) as j:
                for body in bodies:
                    body(j)
            for body in bodies:
                body(UNITS - 1)

        def each_tile(eng, body):
            with eng.Fori(0, NT) as j:
                body(j)

        def cols(b, nt):
            return ds(b * BN, nt * P)

        def tile_cols(j):
            return ds(j * P, P)

        def unit_cols(j):
            return ds(j * P, tiles(j) * P)

        def tile_rows(j):
            return [(j + t, t, LAST_ROWS if tiles(j) > 1 and t else P) for t in range(tiles(j))]

        UNITS = NT - 1
        FIRST_ON_POOL = NT - 4
        SLOT_BLOCKS = [NB // 2 + 1, NB // 2]

        def row(a):
            return a.rearrange("(a n) -> a n", a=1)

        def col(a):
            return a.rearrange("(n a) -> n a", a=1)

        block = ctx.enter_context(nc.Block())

        @block.sync
        def _(sp):
            start_counters(sp, "sp")

            def load_rows(rows, of, s):
                sp.dma_start(rows[:, 0, :], of[0:P * GE].rearrange("(g e) -> g e", e=GE)).then_inc(s, 16)
                sp.dma_start(rows[0:GT - 1, 1, :],
                             of[P * GE:(NG - 1) * GE].rearrange("(g e) -> g e", e=GE)).then_inc(s, 16)
                sp.dma_start(rows[GT - 1:GT, 1, 0:LAST_E], row(of[(NG - 1) * GE:E])).then_inc(s, 16)
                sp.dma_start(rows[GT - 1:GT, 1, LAST_E:GE], row(of[E - (GE - LAST_E):E])).then_inc(s, 16)

            def load_block(b, u, t, nt):
                sp.wait_ge(x_turned, done(b - 2))
                if nt == BT:
                    sp.dma_start(xs[:, u, :, :], x[0:NB * BN, :].rearrange("(n t p) d -> p n t d", t=BT, p=P)
                                 [:, ds(b, 1), :, :].rearrange("p a t d -> p (a t) d")).then_inc(x_in[u], 16)
                else:
                    sp.dma_start(xs[0:LAST_ROWS, u, 0, :], x[NB * BN:N, :]).then_inc(x_in[u], 16)

            def store_A(b, u, t, nt):
                sp.wait_ge(A_made, done(b))
                if nt == BT:
                    sp.dma_start(A_d[0:NB * BN, :].rearrange("(n t p) d -> p n t d", t=BT, p=P)
                                 [:, ds(b, 1), :, :].rearrange("p a t d -> p (a t) d"),
                                 As[:, u, :, :]).then_inc(A_out[u], 16)
                else:
                    sp.dma_start(A_d[NB * BN:NPAD, :], As[:, u, 0, :]).then_inc(A_out[u], 16)

            blocks(sp, (0, load_block), (0, only_at({0: lambda: load_rows(dst_rows, dst, dst_in),
                                                     1: lambda: load_rows(src_rows, src, src_in)})), (3, store_A))

            def load_pair(k, u, t):
                last = is_last(k)
                sp.wait_ge(ohT_made, done(2 * k - 3))
                for h in range(2):
                    to = dst_bc[(1 - h) * W:(2 - h) * W, u, :]
                    if last and h:
                        sp.dma_start(to[:, 0:LAST_E], row(dst[(NG - 1) * GE:E]).to_broadcast([W, LAST_E])) \
                            .then_inc(dst_bc_in[u], 16)
                        sp.dma_start(to[:, LAST_E:GE], no_dst[:, :]).then_inc(dst_bc_in[u], 16)
                    else:
                        sp.dma_start(to, row(dst[ds((2 * k + h) * GE, GE)]).to_broadcast([W, GE])) \
                            .then_inc(dst_bc_in[u], 16)
                sp.wait_ge(ef_turned, done(k - 2))
                to = ef_s[:, u, :].rearrange("p (h f) -> p h f", h=2)
                if last:
                    e0 = 2 * k * GE
                    sp.dma_start(to[:, 0, :], ef[e0:e0 + GE, :].rearrange("(p j) f -> p (j f)", j=CH)) \
                        .then_inc(ef_in[u], 16)
                    sp.dma_start(to[0:LAST_P, 1, :],
                                 ef[e0 + GE:E, :].rearrange("(p j) f -> p (j f)", j=CH)).then_inc(ef_in[u], 16)
                    sp.dma_start(to[LAST_P:P, 1, :],
                                 ef[0:GE - LAST_E, :].rearrange("(p j) f -> p (j f)", j=CH)) \
                        .then_inc(ef_in[u], 16)
                else:
                    sp.dma_start(to, ef[ds(2 * k * GE, 2 * GE), :].rearrange("(h p j) f -> p h (j f)", h=2, j=CH)) \
                        .then_inc(ef_in[u], 16)

            def load_weights():
                for to, of in ((w2[:, :], W2), (w3[:, :, :], W3.rearrange("(h k) n -> k h n", h=2)),
                               (w4[:, :], W4), (v1[:, :], V1), (v2[:, :], V2),
                               (b4_bc[:, :], row(b4).to_broadcast([P, D])),
                               (c2_bc[:, :], row(c2).to_broadcast([P, D])),
                               (gamma_bc[:, :], row(gamma).to_broadcast([P, D])),
                               (beta_bc[:, :], row(beta).to_broadcast([P, D])),
                               (b2_col[:, :], col(b2)), (b3_col[:, :], col(b3)), (c1_col[:, :], col(c1)),
                               (one_eps[:, :], row(eps).to_broadcast([P, 1]))):
                    sp.dma_start(to, of).then_inc(w_in, 16)

            def load_unit0(j):
                sp.wait_ge(xb_made, done(j - 1))
                for tile, t, rows in tile_rows(j):
                    sp.dma_start(xt[0:rows, t, :], x[ds(tile * P, rows), :]).then_inc(xt_in, 16)

            def load_unit1(j):
                sp.wait_ge(y_made, done(j - 1))
                for tile, t, _ in tile_rows(j):
                    sp.dma_start(xt[:, t, :], x1_d[tile_cols(tile), :]).then_inc(x1_in, 16)

            def load_any(i, rows=P):
                sp.wait_ge(any_ef_turned, done(i - 1))
                sp.dma_start(ef_s[0:rows, 0, 0:CH * FE], ef[ds(i * GE, rows * CH), :]
                             .rearrange("(p j) f -> p (j f)", j=CH)).then_inc(any_ef_in, 16)

            def ordered():
                pairs(sp, of_unit(9, load_unit0), (0, load_pair), (0, only_at({1: load_weights})))
                sp.wait_ge(x1_out, landed(NT - 1))
                pairs(sp, of_unit(4, load_unit1))
                sp.wait_ge(o_out, landed(NT - 1))

            def any_order():
                load_weights()
                sp.dma_start(ef_s[:, 0, CH * FE:], ef[0:P * CH, :].rearrange("(p j) f -> p (j f)", j=CH)) \
                    .then_inc(ef_in[0], 16)
                with sp.Fori(0, NG - 1) as i:
                    load_any(i)
                load_any(NG - 1, LAST_P)
                all_units(sp, load_unit0)
                sp.wait_ge(x1_out, landed(NT - 1))
                all_units(sp, load_unit1)
                sp.wait_ge(o_out, landed(NT - 1))

            sp.wait_ge(consts, 1)
            either_order(sp, ordered, any_order)

        @block.gpsimd
        def _(pool):
            start_counters(pool, "pool")
            g = nc.gpsimd
            g.memset(ident[:, :], 0.0).then_inc(id_zero, 1)
            g.memset(ones[:, :], 1.0)
            g.memset(eps_col[:, :], LN_EPS)
            g.memset(mhalf[:, :], -0.5)
            g.memset(xt[:, 1, :], 0.0)
            g.iota(iota_w[:, :], [[1, PW]], base=0, channel_multiplier=0, allow_small_or_imprecise_dtypes=True)
            g.iota(iota_p[:, :], [[0, 1]], base=0, channel_multiplier=1, allow_small_or_imprecise_dtypes=True)
            g.iota(tile_end[:, :].rearrange("p (t h) -> p t h", h=2), [[P, NT], [0, 2]], base=-P,
                   channel_multiplier=0, allow_small_or_imprecise_dtypes=True)
            g.memset(lo[:, :], 0.0)
            g.memset(src_col[:, NG * CH:], 0)
            g.memset(dst_col[:, (NG - 1) * CH:], PAD_DST)
            pool.wait_ge(id_zero, 1)
            g.affine_select(out=ident[:, :], in_=ident[:, :], compare_op=ALU.not_equal, fill=1.0, base=0,
                            pattern=[[-1, P]], channel_multiplier=1).then_inc(consts, 1)

            g.memset(cdeg[:, :], 0.0)
            g.memset(no_dst[:, :], int(PAD_DST))
            pool.wait_ge(own_rows_made, 1)
            pool.wait_ge(wef_in, 16)
            for u in range(2):
                for h in range(2):
                    shape = [P, CH, D]
                    g.tensor_tensor(terms_r[:, u, h, :, :], wef[:, :].unsqueeze(1).to_broadcast(shape),
                                    own_rows[:, h * CH:(h + 1) * CH].unsqueeze(2).to_broadcast(shape),
                                    ALU.mult).then_inc(wef_ready, 1)
            g.memset(S[:, :], 0.0)
            g.memset(T[:, :], 0.0).then_inc(zeroed, 1)

            def gather_rows(table, slot, indices, gathered):
                for j in range(CH):
                    g.indirect_dma_start(
                        out=gath[:, slot, j * D:(j + 1) * D], out_offset=None, in_=table[0:N, :],
                        in_offset=bass.IndirectOffsetOnAxis(ap=indices[:, j:j + 1], axis=0)).then_inc(gathered, 16)

            def gather_pair(table, staged, gathered, used):
                def body(k, u, t):
                    pool.wait_ge(staged, done(k))
                    pool.nop(nofuse=True)
                    for h in range(2):
                        pool.wait_ge(used, done(2 * k + (h - 4)) if used is pre_made else done(k - 2))
                        pool.nop(nofuse=True)
                        gather_rows(table, 2 * u + h, idx[:, u, h * CH:(h + 1) * CH], gathered[2 * u + h])
                return body

            def rsqrt0(j):
                if rsqrt_on_pool(j):
                    pool.wait_ge(mv_made, done(j))
                    pool.nop(nofuse=True)
                    n = tiles(j)
                    g.tensor_scalar_add(var_eps[:, 0:n], mv[:, 0, 0:n, 1], LN_EPS).then_inc(var_eps_made, 1)
                    pool.wait_ge(var_eps_made, done(j - FIRST_ON_POOL))
                    g.tensor_tensor(rstd[:, 0, 0:n], var_eps[:, 0:n], mhalf[:, 0:n],
                                    ALU.pow).then_inc(pool_rstd_made, 1)

            def source_table_stored():
                for u in range(2):
                    pool.wait_ge(A_out[u], 16 * SLOT_BLOCKS[u])

            def ordered():
                source_table_stored()
                pairs(pool, (0, gather_pair(A_d, staged0, gathered0, pre_made)), of_unit(9, rsqrt0))
                pool.wait_ge(x1_out, landed(NT - 1))
                pairs(pool, (0, gather_pair(x1_d, staged1, gathered1, agg_ps)))

            def any_terms(i):
                pool.wait_ge(any_staged, done(i))
                pool.nop(nofuse=True)
                gather_rows(A_d, 0, idx[:, 0, 0:CH], any_src_in)
                gather_rows(B_d, 1, idx[:, 1, 0:CH], any_dst_in)

            def any_rows(i):
                pool.wait_ge(any1_staged, done(i))
                pool.nop(nofuse=True)
                gather_rows(x1_d, 0, idx[:, 0, 0:CH], any1_x1_in)

            def any_order():
                source_table_stored()
                pool.wait_ge(any_b_out, landed(NT - 1))
                all_groups(pool, any_terms)
                pool.wait_ge(x1_out, landed(NT - 1))
                all_groups(pool, any_rows)

            either_order(pool, ordered, any_order)

        @block.scalar
        def _(act):
            start_counters(act, "act")
            a = nc.scalar
            act.dma_start(wab[:, :].rearrange("k (h n) -> k h n", h=2),
                          W1[0:2 * D, :].rearrange("(h k) n -> k h n", h=2)).then_inc(wab_in, 16)
            act.dma_start(wef[:, :], W1[2 * D:2 * D + FE, :].unsqueeze(0)
                          .to_broadcast([P // FE, FE, D])).then_inc(wef_in, 16)
            act.dma_start(b1_bc[:, :], row(b1).to_broadcast([P, D])).then_inc(wab_in, 16)

            def keep_xT(b, u, t, nt):
                act.wait_ge(x_turned, done(b))
                act.wait_ge(ab_ps, done(b - 2))
                act.wait_ge(xT_kept, done(b - 2))
                a.copy(xTs[:, u, 0:nt * P], bank[u][:, 0:nt * P]).then_inc(xTs_made, 1)

            blocks(act, (0, keep_xT))
            act.wait_ge(xT_kept, done(NB))
            act.wait_ge(wef_ready, 4)
            act.wait_ge(base_ready, 1)

            def window_x(k, u, t):
                act.wait_ge(ef_turned, done(k - 1))
                for h in range(2):
                    at = act.value_load(bases[0:1, ds(k, 1), 1 + h], min_val=0, max_val=NPAD - W)
                    last = a.copy(xw[:, (1 - h) * W:(2 - h) * W], xT[:, ds(at, W)])
                last.then_inc(xw_made, 1)

            def edge_features(k, u, t):
                act.wait_ge(ef_turned, done(k))
                act.wait_ge(pre_ps, done(2 * k - 3))
                for h in range(2):
                    r = slice(h * W, (h + 1) * W)
                    a.copy(terms_l[r, u, h, :, :], bank[4][r, 0:P].unsqueeze(1).to_broadcast([W, CH, P]))
                    last = a.copy(terms_r[r, u, 1 - h, :, :], bank[4][r, P:2 * P].unsqueeze(1).to_broadcast([W, CH, P]))
                last.then_inc(efT_made, 1)

            def messages(k, u, t):
                for h in range(2):
                    g = 2 * k + h
                    act.wait_ge(pre_made, done(g))
                    act.wait_ge(sums_ps, done(k - 2))
                    a.activation(msg[:, 2 * u + h, :], pre[:, h, :], ACT.Silu).then_inc(msg_made, 1)

            def hidden0(j):
                act.wait_ge(w_in, 16 * 13)
                act.wait_ge(upd_ps, done(j))
                act.wait_ge(hnew_ps, done(j - 1))
                n = tiles(j) * P
                a.activation(hid[:, 0:n], bank[5][:, 0:n], ACT.Silu, bias=b3_col[:, :]).then_inc(hid_made, 1)

            def std_of(n, variance, used, made):
                def body(j):
                    act.wait_ge(variance, done(j))
                    act.wait_ge(used, done(j - 1))
                    act.nop(nofuse=True)
                    a.activation(std[:, n, 0:tiles(j)], mv[:, n, 0:tiles(j), 1], ACT.Sqrt,
                                 bias=eps_col[:, :]).then_inc(made, 1)
                return body

            std0 = std_of(0, mv_made, rstd_made, std_made)
            std1 = std_of(0, rmv_made, rinv_made, rstd1_made)
            std2 = std_of(1, ymv_made, yinv_made, ystd_made)

            def store0(j):
                act.wait_ge(x1_made, done(j))
                for tile, t, _ in tile_rows(j):
                    act.dma_start(x1_d[tile_cols(tile), :], ot[:, t, :]).then_inc(x1_out, 16)

            def start_T(j):
                act.wait_ge(one_eps_made, 1)
                act.wait_ge(x1_turned, done(j))
                a.activation(T[:, unit_cols(j)], bank[7][:, 0:tiles(j) * P], ACT.Copy,
                             scale=one_eps[:, :]).then_inc(T_init, 1)

            def hidden1(j):
                act.wait_ge(z_ps, done(j))
                act.wait_ge(r_ps, done(j - 1))
                n = tiles(j) * P
                a.activation(hid[:, 0:n], bank[5][:, 0:n], ACT.Relu, bias=c1_col[:, :]).then_inc(z_made, 1)

            def store1(j):
                act.wait_ge(o_made, done(j))
                for tile, t, rows in tile_rows(j):
                    act.dma_start(out[ds(tile * P, rows), :], ot[0:rows, t, :]).then_inc(o_out, 16)

            def ordered():
                pairs(act, of_unit(8, hidden0), of_unit(10, store0), of_unit(11, start_T),
                      (1, edge_features), (0, window_x), (2, messages),
                      of_unit(9, lambda j: None if rsqrt_on_pool(j) else std0(j)))
                pairs(act, of_unit(4, hidden1), of_unit(4, std1), of_unit(4, std2), of_unit(4, store1))

            def any_dst_term(j):
                act.wait_ge(any_b_out, landed(j - 1))
                a.copy(xw[:, :], xT[:, tile_cols(j)]).then_inc(any_xw_made, 1)
                act.wait_ge(any_b_ps, done(j))
                a.copy(any_b[:, :], bank[4][:, P:2 * P]).then_inc(any_b_made, 1)
                act.wait_ge(any_b_made, done(j))
                act.dma_start(B_d[tile_cols(j), :], any_b[:, :]).then_inc(any_b_out, 16)

            def any_messages(i):
                act.wait_ge(any_ef_turned, done(i))
                act.wait_ge(any_pre_ps, done(i - 1))
                a.copy(terms_l[0:W, 0, 0, 0, :], bank[4][0:W, 0:P]).then_inc(any_efT_made, 1)
                act.wait_ge(any_pre_made, done(i))
                act.wait_ge(any_ps, done(i * NT - 1))
                a.activation(msg[:, 0, :], pre[:, 0, :], ACT.Silu).then_inc(any_msg_made, 1)

            def any_order():
                each_tile(act, any_dst_term)
                all_groups(act, any_messages)
                all_units(act, hidden0, std0, store0, start_T)
                all_units(act, hidden1, std1, std2, store1)

            either_order(act, ordered, any_order)

        @block.tensor
        def _(pe):
            start_counters(pe, "pe")
            mm = nc.tensor.matmul

            def turn_rows(rows_f, prep, banks_read, turned):
                pe.wait_ge(prep, 1)
                if banks_read:
                    pe.wait_ge(banks_read, 1)
                for q, n in ((0, P), (1, GT)):
                    for j in range(CH):
                        last = nc.tensor.transpose(
                            bank[6 + q][:, j * P:j * P + n],
                            rows_f[0:n, q, :].rearrange("g (p j) -> g j p", j=CH)[:, j, :], ident[0:n, 0:n])
                last.then_inc(turned, 1)

            pe.wait_ge(consts, 1)
            pe.wait_ge(wab_in, 16 * 2)

            def turn_x(b, u, t, nt):
                pe.wait_ge(x_in[u], 16 * (t + 1))
                pe.wait_ge(xTs_made, done(b - 2))
                for j in range(nt):
                    last = nc.tensor.transpose(bank[u][:, j * P:(j + 1) * P], xs[:, u, j, :], ident[:, :])
                last.then_inc(x_turned, 1)

            def terms(b, u, t, nt):
                pe.wait_ge(xTs_made, done(b))
                pe.wait_ge(A_made, done(b - 2))
                for j in range(nt):
                    last = mm(bank[2 + u][:, j * D:(j + 1) * D], xTs[:, u, j * P:(j + 1) * P], wab[:, 0:D],
                              start=True, stop=True)
                last.then_inc(ab_ps, 1)

            def spread_bases():
                pe.wait_ge(diag_made, 1)
                pe.wait_ge(dst_ready, 1)
                mm(bank[6][:, 0:2 * P], ones[:, :], base_diag[:, :, :].rearrange("p q g -> p (q g)"),
                   start=True, stop=True).then_inc(base_turned, 1)

            def sum_misfits():
                pe.wait_ge(misfits_made, 2)
                mm(bank[7][0:1, 0:2], ones[:, 0:1], misfits[:, :], start=True, stop=True).then_inc(misfits_summed, 1)

            blocks(pe, (0, turn_x), (1, terms), (0, only_at({
                1: lambda: turn_rows(dst_rows_f, dst_prep, None, dst_turned), 2: spread_bases,
                NB: lambda: turn_rows(src_rows_f, src_prep, order_known, src_turned)})),
                   (3, only_at({2: sum_misfits})))
            pe.wait_ge(A_made, done(NB))
            pe.wait_ge(src_ready, 1)
            pe.wait_ge(wef_ready, 4)
            pe.wait_ge(xT_kept, done(NB))

            def weight_products():
                pe.wait_ge(w_in, 16 * 13)
                nc.tensor.transpose(bank[7][:, 0:D], w2[:, :], ident[:, :]).then_inc(w2_turned, 1)
                pe.wait_ge(w2_ready, 1)
                mm(bank[7][:, D:2 * D], w2t[:, :], w3[:, 1, :], start=True, stop=True)
                mm(bank[7][0:1, 2 * D:3 * D], b2_col[:, :], w3[:, 1, :], start=True, stop=True).then_inc(w23_ps, 1)
                pe.wait_ge(w23_ready, 1)

            def turn_ef(k, u, t):
                pe.wait_ge(ef_in[u], 16 * (t + 1) if not is_last(k) else 16 * (t + 3))
                pe.wait_ge(efT_made, done(k - 1))
                nc.tensor.transpose(bank[4][:, 0:P], ef_s[:, u, :], ident[:, :])
                pe.wait_ge(xw_made, done(k))
                mm(bank[4][:, P:2 * P], xw[:, :], wab[:, D:2 * D], start=True, stop=True).then_inc(ef_turned, 1)

            def pre_sums(k, u, t):
                pe.wait_ge(efT_made, done(k))
                pe.wait_ge(ohT_made, done(2 * k + 1))
                for h in range(2):
                    pe.wait_ge(pre_made, done(2 * k + h - 2))
                    for j in range(CH):
                        last = mm(bank[h][:, j * D:(j + 1) * D], terms_l[:, u, h, j, :], terms_r[:, u, h, j, :],
                                  start=True, stop=True)
                    last.then_inc(pre_ps, 1)

            def message_sums(k, u, t):
                pe.wait_ge(sums_added, done(k - 2))
                for c in range(2 * CH):
                    if c % CH == 0:
                        pe.wait_ge(msg_made, done(2 * k + c // CH))
                    mm(bank[2 + u][:, 0:PW], msg[:, 2 * u + c // CH, c % CH * D:(c % CH + 1) * D], oh[:, u, c, :],
                       start=c == 0, stop=c == 2 * CH - 1)
                mm(bank[2 + u][0:1, PW:2 * PW], deg_col[:, u:u + 1], ident[:, :],
                   start=True, stop=True).then_inc(sums_ps, 1)

            def hidden0(j):
                pe.wait_ge(hid_made, done(j - 1))
                at, n = unit_cols(j), tiles(j) * P
                mm(bank[5][:, 0:n], w3[:, 0, :], xT[:, at], start=True, stop=False)
                mm(bank[5][:, 0:n], w23[:, :], S[:, at], start=False, stop=False)
                mm(bank[5][:, 0:n], cdeg[:, :], T[:, at], start=False, stop=True).then_inc(upd_ps, 1)

            def ordered_hidden0(j):
                pe.wait_ge(sums_added, done(last_pair(j)))
                hidden0(j)

            def out0(j):
                pe.wait_ge(hid_made, done(j))
                pe.wait_ge(v_made, done(j - 1))
                for t in range(tiles(j)):
                    last = mm(bank[6][:, t * D:(t + 1) * D], hid[:, t * P:(t + 1) * P], w4[:, :],
                              start=True, stop=True)
                last.then_inc(hnew_ps, 1)

            def turn_x1(j):
                pe.wait_ge(x1_made, done(j))
                pe.wait_ge(T_init, done(j - 1))
                for t in range(tiles(j)):
                    last = nc.tensor.transpose(bank[7][:, t * P:(t + 1) * P], ot[:, t, :], ident[:, :])
                last.then_inc(x1_turned, 1)

            def neighbour_sums(k, u, t):
                pe.wait_ge(oh1_made, done(k))
                pe.wait_ge(agg_added, done(k - 2))
                for c in range(2 * CH):
                    s = 2 * u + c // CH
                    if c % CH == 0:
                        pe.wait_ge(gathered1[s], 16 * CH * (t + 1))
                    last = mm(bank[2 + u][:, 0:PW], gath[:, s, c % CH * D:(c % CH + 1) * D], oh[:, u, c, :],
                              start=c == 0, stop=c == 2 * CH - 1)
                last.then_inc(agg_ps, 1)

            def hidden1(j):
                pe.wait_ge(z_made, done(j - 1))
                mm(bank[5][:, 0:tiles(j) * P], v1[:, :], T[:, unit_cols(j)], start=True, stop=True).then_inc(z_ps, 1)

            def ordered_hidden1(j):
                pe.wait_ge(agg_added, done(last_pair(j)))
                hidden1(j)

            def out1(j):
                pe.wait_ge(z_made, done(j))
                pe.wait_ge(r_made, done(j - 1))
                for t in range(tiles(j)):
                    last = mm(bank[6][:, t * D:(t + 1) * D], hid[:, t * P:(t + 1) * P], v2[:, :],
                              start=True, stop=True)
                last.then_inc(r_ps, 1)

            def ordered():
                pairs(pe, (1, turn_ef), (2, pre_sums), (3, message_sums),
                      (0, only_at({4: weight_products})),
                      of_unit(10, turn_x1), of_unit(8, out0), of_unit(7, ordered_hidden0))
                pairs(pe, of_unit(4, ordered_hidden1), of_unit(4, out1), (0, neighbour_sums))

            def any_dst_term(j):
                pe.wait_ge(any_xw_made, done(j))
                pe.wait_ge(any_b_made, done(j - 1))
                mm(bank[4][:, P:2 * P], xw[:, :], wab[:, D:2 * D], start=True, stop=True).then_inc(any_b_ps, 1)

            def any_pre(i):
                pe.wait_ge(any_ef_in, landed(i))
                pe.wait_ge(any_efT_made, done(i - 1))
                nc.tensor.transpose(bank[4][:, 0:P], ef_s[:, 0, :], ident[:, :]).then_inc(any_ef_turned, 1)
                pe.wait_ge(any_efT_made, done(i))
                pe.wait_ge(any_pre_made, done(i - 1))
                mm(bank[0][:, :], terms_l[0:W, 0, 0, 0, :], terms_r[0:W, 0, 0, :, :].rearrange("k j d -> k (j d)"),
                   start=True, stop=True).then_inc(any_pre_ps, 1)
                pe.wait_ge(any_msg_made, done(i))
                pe.nop(nofuse=True)

            def any_gathered(i):
                pe.wait_ge(any1_x1_in, 16 * CH * (i + 1))
                pe.nop(nofuse=True)

            def any_sums(rows, oh_ready, added, summed, n):
                pe.wait_ge(oh_ready, done(n))
                pe.wait_ge(added, done(n - 1))
                for j in range(CH):
                    mm(bank[2][:, 0:P], rows[:, 0, j * D:(j + 1) * D], oh[:, 0, j, :],
                       start=j == 0, stop=j == CH - 1)
                for j in range(CH):
                    last = mm(bank[2][0:1, P:2 * P], ones[:, 0:1], oh[:, 0, j, :], start=j == 0, stop=j == CH - 1)
                last.then_inc(summed, 1)

            def any_order():
                weight_products()
                each_tile(pe, any_dst_term)
                pe.wait_ge(any_b_made, done(NT - 1))
                pe.wait_ge(ef_in[0], 16)
                all_groups(pe, any_pre, lambda w, n: any_sums(msg, any_oh_made, any_added, any_ps, n))
                pe.wait_ge(any_added, done(NG * NT - 1))
                all_units(pe, hidden0, out0, turn_x1)
                all_groups(pe, any_gathered, lambda w, n: any_sums(gath, any1_oh_made, any1_added, any1_ps, n))
                pe.wait_ge(any1_added, done(NG * NT - 1))
                all_units(pe, hidden1, out1)

            either_order(pe, ordered, any_order)

        @block.vector
        def _(dve):
            start_counters(dve, "dve")
            ve_ = nc.vector

            def cols_of(turned, column, last_p):
                dve.wait_ge(turned, 1)
                for q, g0, n in ((0, 0, P), (1, P, GT - 1)):
                    ps = bank[6 + q][:, :].rearrange("p (j g) -> p g j", j=CH)
                    ve_.tensor_copy(column[:, g0 * CH:(g0 + n) * CH].rearrange("p (g j) -> p g j", j=CH),
                                    ps[:, 0:n, :])
                return ve_.tensor_copy(column[0:last_p, (NG - 1) * CH:NG * CH], ps[0:last_p, n, :])

            def to_float(rows, rows_f, landed, made):
                dve.wait_ge(landed, 16 * 4)
                ve_.tensor_copy(rows_f[:, 0, :], rows[:, 0, :])
                ve_.tensor_copy(rows_f[0:GT, 1, :], rows[0:GT, 1, :]).then_inc(made, 1)

            def keep_A(b, u, t, nt):
                dve.wait_ge(ab_ps, done(b))
                if again(t):
                    dve.wait_ge(A_out[u], 16 * t)
                ve_.tensor_tensor(As[:, u, 0:nt, :], bank[2 + u][:, 0:nt * D].rearrange("p (t d) -> p t d", d=D),
                                  b1_bc[:, :].unsqueeze(1).to_broadcast([P, nt, D]), ALU.add).then_inc(A_made, 1)

            def keep_xT(b, u, t, nt):
                dve.wait_ge(xTs_made, done(b))
                ve_.tensor_copy(xT[:, cols(b, nt)], xTs[:, u, 0:nt * P]).then_inc(xT_kept, 1)

            by_pair = base_bc[:, 0:NG].rearrange("p (k h) -> p k h", h=2)

            def least_dst():
                to_float(dst_rows, dst_rows_f, dst_in, dst_prep)
                dve.wait_ge(dst_prep, 1)
                dve.wait_ge(consts, 1)
                ve_.tensor_reduce(lo[:, 0:1], dst_rows_f[:, 0, :], AX_X, ALU.min)
                ve_.tensor_reduce(lo[0:GT, 1:2], dst_rows_f[0:GT, 1, :], AX_X, ALU.min).then_inc(lo_made, 1)
                dve.wait_ge(lo_made, 1)
                for q in range(2):
                    last = ve_.tensor_scalar(base_diag[:, q, :], ident[:, :], lo[:, q:q + 1], float(NPAD),
                                             ALU.mult, ALU.min)
                last.then_inc(diag_made, 1)

            def window_bases():
                cols_of(dst_turned, dst_col, LAST_P).then_inc(dst_ready, 1)
                dve.wait_ge(base_turned, 1)
                ve_.tensor_copy(base_bc[:, :], bank[6][:, 0:2 * P]).then_inc(base_steps, 1)
                dve.wait_ge(base_steps, 1)
                ve_.tensor_tensor(pair_bc[:, :], by_pair[:, :, 0], by_pair[:, :, 1], ALU.min).then_inc(base_steps, 1)
                dve.wait_ge(base_steps, 2)
                ve_.tensor_scalar(pair_bc[:, :], pair_bc[:, :], float(NPAD - PW), None, ALU.min) \
                    .then_inc(base_steps, 1)
                dve.wait_ge(base_steps, 3)
                ve_.scalar_tensor_tensor(out=by_pair, in0=pair_bc[:, :].unsqueeze(2).to_broadcast([P, NPAIR, 2]),
                                         scalar=float(W), in1=by_pair, op0=ALU.add, op1=ALU.min) \
                    .then_inc(base_steps, 1)
                ve_.tensor_copy(bases[:, :, 0], pair_bc[0:1, :])
                dve.wait_ge(base_steps, 4)
                for h in range(2):
                    last = ve_.tensor_copy(bases[:, :, 1 + h], by_pair[0:1, :, h])
                last.then_inc(base_ready, 1)

            def find_misfits():
                dve.wait_ge(dst_ready, 1)
                ve_.tensor_tensor(past[:, :].rearrange("p (g j) -> p g j", j=CH),
                                  dst_col[:, :].rearrange("p (g j) -> p g j", j=CH),
                                  base_bc[:, 0:NG].unsqueeze(2).to_broadcast([P, NG, CH]),
                                  ALU.subtract).then_inc(past_made, 1)
                ve_.tensor_tensor(early[:, :], tile_end[:, :], pair_bc[:, :], ALU.subtract).then_inc(early_made, 1)
                dve.wait_ge(past_made, 1)
                ve_.tensor_scalar(past[:, :], past[:, :], float(W), None, ALU.is_ge, ALU.add,
                                  accum_out=misfits[:, 0:1]).then_inc(misfits_made, 1)
                dve.wait_ge(early_made, 1)
                ve_.tensor_scalar(early[:, :], early[:, :], 0.0, None, ALU.is_gt, ALU.add,
                                  accum_out=misfits[:, 1:2]).then_inc(misfits_made, 1)

            def relative_dst():
                dve.wait_ge(misfits_summed, 1)
                ve_.tensor_copy(misfit_count[:, :], bank[7][0:1, 0:2]).then_inc(order_known, 1)
                ve_.tensor_tensor(dst_rel[:, :].rearrange("p (k c) -> p k c", c=2 * CH),
                                  dst_col[:, :].rearrange("p (k c) -> p k c", c=2 * CH),
                                  pair_bc[:, :].unsqueeze(2).to_broadcast([P, NPAIR, 2 * CH]), ALU.subtract)
                for h in range(2):
                    r = slice((1 - h) * W, (2 - h) * W)
                    last = ve_.tensor_scalar(node_col[r, :], by_pair[r, :, h], iota_p[r, :], float((h - 1) * W),
                                             ALU.add, ALU.add)
                last.then_inc(rel_ready, 1)
                to_float(src_rows, src_rows_f, src_in, src_prep)

            def stage(k, u, staged):
                ve_.tensor_copy(idx[:, u, :], src_col[:, ds(k * (2 * CH), 2 * CH)]).then_inc(staged, 1)

            dve.wait_ge(consts, 1)
            ve_.tensor_reduce(own_rows[:, :], ident[:, :].rearrange("p (q f) -> p q f", f=FE), AX_X,
                              ALU.add).then_inc(own_rows_made, 1)
            least_dst()
            dve.wait_ge(wab_in, 16 * 2)
            blocks(dve, (1, keep_A),
                   (0, only_at({NB: lambda: cols_of(src_turned, src_col, P).then_inc(src_ready, 1)})),
                   (1, keep_xT), (0, only_at({1: window_bases, 3: find_misfits})), (5, only_at({1: relative_dst})))

            dve.wait_ge(src_ready, 1)
            for u in range(2):
                stage(u, u, staged0)
            dve.wait_ge(rel_ready, 1)
            dve.wait_ge(zeroed, 1)
            def weight_products():
                dve.wait_ge(w_in, 16 * 13)
                ve_.tensor_scalar_add(one_eps[:, :], one_eps[:, :], 1.0).then_inc(one_eps_made, 1)
                dve.wait_ge(w2_turned, 1)
                ve_.tensor_copy(w2t[:, :], bank[7][:, 0:D]).then_inc(w2_ready, 1)
                dve.wait_ge(w23_ps, 1)
                ve_.tensor_copy(w23[:, :], bank[7][:, D:2 * D])
                dve.wait_ge(zeroed, 1)
                ve_.tensor_copy(cdeg[0:1, :], bank[7][0:1, 2 * D:3 * D]).then_inc(w23_ready, 1)

            def one_hots(read, made):
                def body(k, u, t):
                    dve.wait_ge(read, done(k - 2))
                    shape = [P, 2 * CH, PW]
                    ve_.tensor_tensor(oh[:, u, :, :], iota_w[:, :].unsqueeze(1).to_broadcast(shape),
                                      dst_rel[:, ds(k * (2 * CH), 2 * CH)].unsqueeze(2).to_broadcast(shape),
                                      ALU.is_equal).then_inc(made, 1)
                return body

            def windows(k, u, t):
                dve.wait_ge(dst_bc_in[u], 32 * (t + 1) + (16 if is_last(k) else 0))
                dve.wait_ge(pre_ps, done(2 * k - 3))
                dve.wait_ge(sums_ps, done(k - 2))
                for h in range(2):
                    r = slice((1 - h) * W, (2 - h) * W)
                    ve_.tensor_scalar(terms_l[r, u, h, :, :],
                                      dst_bc[r, u, :].rearrange("n (p j) -> n j p", j=CH), node_col[r, ds(k, 1)],
                                      None, ALU.is_equal, ALU.add, accum_out=deg_col[r, u:u + 1]).then_inc(ohT_made, 1)

            def source_terms(k, u, t):
                for h in range(2):
                    g = 2 * k + h
                    s = 2 * u + h
                    dve.wait_ge(gathered0[s], 16 * CH * (t + 1))
                    dve.wait_ge(pre_ps, done(g))
                    dve.wait_ge(msg_made, done(g - 2))
                    ve_.tensor_tensor(pre[:, h, :], bank[h][:, :], gath[:, s, :], ALU.add).then_inc(pre_made, 1)
                stage(k + 2, u, staged0)

            def add_sums(k, u, t):
                at, at0, at1 = [dve.value_load(bases[0:1, ds(k, 1), i], min_val=0, max_val=NPAD - (W if i else PW))
                                for i in range(3)]
                dve.wait_ge(sums_ps, done(k))
                dve.wait_ge(sums_added, done(k - 1))
                ve_.tensor_tensor(S[:, ds(at, PW)], S[:, ds(at, PW)], bank[2 + u][:, 0:PW], ALU.add)
                ve_.tensor_tensor(T[0:1, ds(at0, W)], T[0:1, ds(at0, W)],
                                  bank[2 + u][0:1, PW + W:2 * PW], ALU.add).then_inc(deg_added, 1)
                dve.wait_ge(deg_added, done(k))
                ve_.tensor_tensor(T[0:1, ds(at1, W)], T[0:1, ds(at1, W)],
                                  bank[2 + u][0:1, PW:PW + W], ALU.add).then_inc(sums_added, 1)

            def add_neighbours(k, u, t):
                at = dve.value_load(bases[0:1, ds(k, 1), 0], min_val=0, max_val=NPAD - PW)
                dve.wait_ge(agg_ps, done(k))
                dve.wait_ge(agg_added, done(k - 1))
                ve_.tensor_tensor(T[:, ds(at, PW)], T[:, ds(at, PW)], bank[2 + u][:, 0:PW],
                                  ALU.add).then_inc(agg_added, 1)
                stage(k + 2, u, staged1)

            def stats(j, n, of, read, raw, made):
                dve.wait_ge(read, done(j))
                dve.wait_ge(made, done(j - 1))
                for t in range(tiles(j)):
                    last = ve_.bn_stats(st[:, n, t, :], of[:, t, :])
                last.then_inc(raw, 1)
                dve.wait_ge(raw, done(j))
                dve.nop(nofuse=True)
                for t in range(tiles(j)):
                    last = ve_.bn_aggr(mv[:, n, t, :], st[:, n, t, :])
                last.then_inc(made, 1)

            def invert(j, n, made, inverted):
                dve.wait_ge(made, done(j))
                ve_.reciprocal(rstd[:, n, 0:tiles(j)], std[:, n, 0:tiles(j)]).then_inc(inverted, 1)
                dve.wait_ge(inverted, done(j))
                dve.nop(nofuse=True)

            def normalise(j, n, of, made):
                for t in range(tiles(j)):
                    last = ve_.tensor_scalar(ot[:, t, :], of[:, t, :], mv[:, n, t, 0:1], rstd[:, n, t:t + 1],
                                             ALU.subtract, ALU.mult)
                last.then_inc(made, 1)

            def of_bank(j):
                return bank[6][:, 0:tiles(j) * D].rearrange("p (t d) -> p t d", d=D)

            def every_row(j, row_bc):
                return row_bc[:, :].unsqueeze(1).to_broadcast([P, tiles(j), D])

            def rows0(j):
                n = slice(0, tiles(j))
                dve.wait_ge(xt_in, moved(j))
                dve.wait_ge(x1_made, done(j - 1))
                ve_.scalar_tensor_tensor(out=v[:, n, :], in0=xt[:, n, :], scalar=2.0, in1=every_row(j, b4_bc),
                                         op0=ALU.mult, op1=ALU.add).then_inc(xb_made, 1)
                dve.wait_ge(xb_made, done(j))
                dve.wait_ge(hnew_ps, done(j))
                ve_.tensor_tensor(v[:, n, :], of_bank(j), v[:, n, :], ALU.add).then_inc(v_made, 1)
                stats(j, 0, v, v_made, st_made, mv_made)

            def ordered_norm0(j):
                if rsqrt_on_pool(j):
                    dve.wait_ge(pool_rstd_made, done(j - FIRST_ON_POOL))
                    normalise0(j)
                else:
                    norm0(j)

            def norm0(j):
                invert(j, 0, std_made, rstd_made)
                normalise0(j)

            def normalise0(j):
                dve.wait_ge(x1_out, landed(j - 1))
                dve.wait_ge(x1_turned, done(j - 1))
                normalise(j, 0, v, x1_made)

            def rows1(j):
                n = slice(0, tiles(j))
                dve.wait_ge(x1_in, moved(j))
                ve_.tensor_tensor(v[:, n, :], xt[:, n, :], every_row(j, c2_bc), ALU.add).then_inc(rb_made, 1)
                dve.wait_ge(rb_made, done(j))
                dve.wait_ge(r_ps, done(j))
                ve_.tensor_tensor(v[:, n, :], of_bank(j), v[:, n, :], ALU.add).then_inc(r_made, 1)
                stats(j, 0, v, r_made, rst_made, rmv_made)

            def norm1(j):
                invert(j, 0, rstd1_made, rinv_made)
                for t in range(tiles(j)):
                    last = ve_.scalar_tensor_tensor(out=nrm[:, 0, t, :], in0=v[:, t, :], scalar=mv[:, 0, t, 0:1],
                                                    in1=gamma_bc[:, :], op0=ALU.subtract, op1=ALU.mult)
                last.then_inc(rg_made, 1)
                dve.wait_ge(rg_made, done(j))
                dve.nop(nofuse=True)
                for t in range(tiles(j)):
                    last = ve_.scalar_tensor_tensor(out=nrm[:, 1, t, :], in0=nrm[:, 0, t, :],
                                                    scalar=rstd[:, 0, t:t + 1], in1=beta_bc[:, :],
                                                    op0=ALU.mult, op1=ALU.add)
                last.then_inc(rh_made, 1)
                dve.wait_ge(rh_made, done(j))
                dve.wait_ge(o_made, done(j - 1))
                n = slice(0, tiles(j))
                ve_.scalar_tensor_tensor(out=y[:, n, :], in0=nrm[:, 1, n, :], scalar=0.0, in1=xt[:, n, :],
                                         op0=ALU.max, op1=ALU.add).then_inc(y_made, 1)
                stats(j, 1, y, y_made, yst_made, ymv_made)

            def norm2(j):
                invert(j, 1, ystd_made, yinv_made)
                dve.wait_ge(o_out, landed(j - 1))
                normalise(j, 1, y, o_made)

            def ordered():
                pairs(dve, (0, only_at({5: weight_products})), of_unit(9, rows0),
                      (2, source_terms), (1, windows), (1, one_hots(sums_ps, oh_made)),
                      (3, add_sums), of_unit(9, ordered_norm0))
                for u in range(2):
                    stage(u, u, staged1)
                dve.wait_ge(T_init, done(UNITS - 1))
                dve.wait_ge(x1_out, landed(NT - 1))
                pairs(dve, (0, one_hots(agg_ps, oh1_made)), of_unit(4, rows1), of_unit(4, norm1), of_unit(4, norm2),
                      (0, add_neighbours))

            def pick(i, before, copied, staged):
                dve.wait_ge(before, done(i * NT - 1))
                at = ds(i * CH, CH)
                ve_.tensor_copy(any_rel[:, :], dst_col[:, at]).then_inc(copied, 1)
                ve_.tensor_copy(idx[:, 0, 0:CH], src_col[:, at])
                dve.wait_ge(copied, done(i))
                ve_.tensor_scalar_max(idx[:, 1, 0:CH], any_rel[:, :], 0.0).then_inc(staged, 1)

            def add_tile(w, n, moved, oh_ready, summed, added, layer):
                dve.wait_ge(moved, done(n - 1))
                dve.wait_ge(summed, done(n - 1))
                shape = [P, CH, P]
                ve_.tensor_tensor(oh[:, 0, 0:CH, :], iota_w[:, :].unsqueeze(1).to_broadcast(shape),
                                  any_rel[:, :].unsqueeze(2).to_broadcast(shape),
                                  ALU.is_equal).then_inc(oh_ready, 1)
                dve.wait_ge(oh_ready, done(n))
                ve_.tensor_scalar_add(any_rel[:, :], any_rel[:, :], -float(P)).then_inc(moved, 1)
                dve.wait_ge(summed, done(n))
                at = tile_cols(w)
                if layer == 0:
                    ve_.tensor_tensor(T[0:1, at], T[0:1, at], bank[2][0:1, P:2 * P], ALU.add)
                to = T if layer else S
                ve_.tensor_tensor(to[:, at], to[:, at], bank[2][:, 0:P], ALU.add).then_inc(added, 1)

            def any_terms(i):
                pick(i, any_moved, any_copied, any_staged)
                dve.wait_ge(any_src_in, 16 * CH * (i + 1))
                dve.wait_ge(any_dst_in, 16 * CH * (i + 1))
                dve.wait_ge(any_msg_made, done(i - 1))
                ve_.tensor_tensor(pre[:, 0, :], gath[:, 0, :], gath[:, 1, :], ALU.add).then_inc(any_ab_made, 1)
                dve.wait_ge(any_ab_made, done(i))
                dve.wait_ge(any_pre_ps, done(i))
                ve_.tensor_tensor(pre[:, 0, :], bank[0][:, :], pre[:, 0, :], ALU.add).then_inc(any_pre_made, 1)

            def any_order():
                weight_products()
                all_groups(dve, any_terms, lambda w, n: add_tile(
                    w, n, any_moved, any_oh_made, any_ps, any_added, 0))
                all_units(dve, rows0, norm0)
                dve.wait_ge(T_init, done(UNITS - 1))
                dve.wait_ge(x1_out, landed(NT - 1))
                all_groups(dve, lambda i: pick(i, any1_moved, any1_copied, any1_staged), lambda w, n: add_tile(
                    w, n, any1_moved, any1_oh_made, any1_ps, any1_added, 1))
                all_units(dve, rows1, norm1, norm2)

            either_order(dve, ordered, any_order)


_INS = ['x', 'src', 'dst', 'edge_attr_16', 'L0_gnn_W1', 'L0_gnn_b1', 'L0_gnn_W2', 'L0_gnn_b2', 'L0_gnn_W3',
        'L0_gnn_b3', 'L0_gnn_W4', 'L0_gnn_b4', 'L1_gnn_eps', 'L1_gnn_W1', 'L1_gnn_b1', 'L1_gnn_W2', 'L1_gnn_b2',
        'L1_gnn_gamma', 'L1_gnn_beta']


def kernel(**inputs):
    import numpy as np
    import concourse.bacc as bacc
    from concourse.bass_utils import run_bass_kernel_spmd

    nc = bacc.Bacc("TRN2", target_bir_lowering=False, num_devices=1)
    arrays, args = {}, []
    for name in _INS:
        a = np.ascontiguousarray(inputs[name])
        if a.ndim == 0:
            a = a.reshape(1)
        arrays[f"in_{name}"] = a
        args.append(nc.dram_tensor(f"in_{name}", a.shape, mybir.dt.from_np(a.dtype), kind="ExternalInput").ap())
    out = nc.dram_tensor("out", tuple(inputs["x"].shape), F32, kind="ExternalOutput").ap()
    build(nc, *args, out)
    r = run_bass_kernel_spmd(nc, [arrays], core_ids=[0])
    return r.results[0]["out"]
```
